# Optimizing a Trainium2 kernel written in Bass

```python
import numpy as np
import jax
import jax.numpy as jnp

def _softmax(x, axis=-1):
    return jax.nn.softmax(x, axis=axis)

def _gelu(x):
    return jax.nn.gelu(x, approximate=True)

def _silu(x):
    return jax.nn.silu(x)

def _sigmoid(x):
    return jax.nn.sigmoid(x)

def _layernorm(x, axis=-1, eps=1e-05):
    m = jnp.mean(x, axis=axis, keepdims=True)
    v = jnp.var(x, axis=axis, keepdims=True)
    return (x - m) / jnp.sqrt(v + eps)

def _scatter_add(tgt, idx, src, axis=0):
    return tgt.at[idx].add(src)

def _segment_sum(src, seg, n):
    return jax.ops.segment_sum(src, seg, n)
kernel_name = 'mk_adj_resnorm_d4_adj_r2_3d5e64'

def setup_inputs(seed: int=0):
    np.random.seed(seed)
    _w = jnp.asarray

    def _rec_inputs():
        import jax
        import jax.numpy as jnp
        _gk = jax.random.key(seed)
        x = 7.22e-05 + 1 * jax.random.normal(jax.random.fold_in(_gk, 1), (32, 256, 256), jnp.float32)
        _w = (1.0 + jnp.arange(256, dtype=jnp.float32)) ** (-0.5)
        _w = _w / _w.mean()
        _pij = jnp.clip(0.0625 * _w[:, None] * _w[None, :], 0.0, 1.0)
        _a = jax.random.uniform(jax.random.fold_in(_gk, 2), (32, 256, 256)) < _pij
        _a = jnp.logical_or(_a, jnp.swapaxes(_a, -1, -2))
        _a = jnp.logical_or(_a, jnp.eye(256, dtype=bool))
        _af = _a.astype(jnp.float32)
        _af = _af * jax.random.uniform(jax.random.fold_in(_gk, 3), (32, 256, 256), jnp.float32, 0.05, 1)
        adj = _af
        return (x, adj)
    x, adj = _rec_inputs()

    def _L0_gnn_setup():
        import jax, jax.numpy as jnp
        import numpy as np
        EPS_LN = 1e-05

        def hypergraph_conv(x, adj, W, b):
            N, C, _ = adj.shape
            H = (adj != 0).astype(x.dtype)
            w = adj.reshape(N, -1)[:, :C]
            xw = jnp.einsum('ncd,hd->nch', x, W)
            Dn = jnp.einsum('nce,ne->nc', H, w)
            Dn = jnp.where(Dn > 0, 1.0 / Dn, 0.0)
            Be = H.sum(axis=1)
            Be = jnp.where(Be > 0, 1.0 / Be, 0.0)
            m = Be[:, :, None] * jnp.einsum('nce,nch->neh', H, xw)
            out = Dn[:, :, None] * jnp.einsum('nce,neh->nch', H, m)
            return out + b

        def layer_norm(x, g, b):
            mu = jnp.mean(x, axis=-1, keepdims=True)
            var = jnp.var(x, axis=-1, keepdims=True)
            return (x - mu) * jax.lax.rsqrt(var + EPS_LN) * g + b
        key = jax.random.key(seed)
        ks = jax.random.split(key, 4)
        N, C, Din, Dh, Dout = (16, 512, 256, 512, 256)
        x = jax.random.normal(ks[0], (N, C, Din), dtype=jnp.float32)
        adj = jax.random.uniform(ks[1], (N, C, C), dtype=jnp.float32, minval=0.1, maxval=1.0)
        W1 = jax.random.normal(ks[2], (Dh, Din), dtype=jnp.float32) * (1.0 / np.sqrt(Din))
        b1 = jnp.zeros((Dh,), dtype=jnp.float32)
        gamma = jnp.ones((Dh,), dtype=jnp.float32)
        beta = jnp.zeros((Dh,), dtype=jnp.float32)
        W2 = jax.random.normal(ks[3], (Dout, Dh), dtype=jnp.float32) * (1.0 / np.sqrt(Dh))
        b2 = jnp.zeros((Dout,), dtype=jnp.float32)
        return {'x': x, 'adj': adj, 'W1': W1, 'b1': b1, 'gamma': gamma, 'beta': beta, 'W2': W2, 'b2': b2}
    _L0_gnn_all = _L0_gnn_setup()
    _L0_gnn_in = {k: v for k, v in _L0_gnn_all.items() if k in ('W1', 'b1', 'gamma', 'beta', 'W2', 'b2')}
    del _L0_gnn_all

    def _L1_gnn_setup():
        import jax, jax.numpy as jnp
        import numpy as np
        B, N, F_IN, F_HID, F_OUT = (32, 512, 256, 256, 256)

        def _gcn_layer(x, adj, W, b):
            support = jnp.einsum('bnf,fh->bnh', x, W)
            return jnp.einsum('bnm,bmh->bnh', adj, support) + b
        key = jax.random.key(seed)
        ks = jax.random.split(key, 8)

        def xavier(k, fan_in, fan_out):
            bound = float(np.sqrt(6.0 / (fan_in + fan_out)))
            return jax.random.uniform(k, (fan_in, fan_out), jnp.float32, -bound, bound)
        return {'batch_graph': jax.random.normal(ks[0], (B, N, F_IN), jnp.float32), 'adj': jax.random.uniform(ks[1], (B, N, N), jnp.float32), 'W1': xavier(ks[2], F_IN, F_HID), 'b1': jnp.zeros((F_HID,), jnp.float32), 'W2': xavier(ks[3], F_HID, F_HID), 'b2': jnp.zeros((F_HID,), jnp.float32), 'W3': xavier(ks[4], F_HID, F_OUT), 'b3': jnp.zeros((F_OUT,), jnp.float32)}
    _L1_gnn_all = _L1_gnn_setup()
    _L1_gnn_in = {k: v for k, v in _L1_gnn_all.items() if k in ('W1', 'b1', 'W2', 'b2', 'W3', 'b3')}
    del _L1_gnn_all

    def _L2_gnn_setup():
        import jax, jax.numpy as jnp
        import numpy as np
        EPS = 1e-06
        key = jax.random.key(seed)
        k1, k2, k3 = jax.random.split(key, 3)
        B, N, F, O = (8, 2048, 256, 256)
        x = jax.random.normal(k1, (B, N, F), dtype=jnp.float32)
        adj = jax.random.uniform(k2, (B, N, N), dtype=jnp.float32)
        W = jax.random.normal(k3, (O, 2 * F), dtype=jnp.float32) * (1.0 / np.sqrt(2 * F))
        return {'x': x, 'adj': adj, 'W': W}
    _L2_gnn_all = _L2_gnn_setup()
    _L2_gnn_in = {k: v for k, v in _L2_gnn_all.items() if k in ('W',)}
    del _L2_gnn_all

    def _L3_gnn_setup():
        import jax, jax.numpy as jnp
        import numpy as np
        B, N, D_IN, D_OUT = (4, 2048, 256, 256)
        key = jax.random.key(seed)
        k1, k2, k3, k4 = jax.random.split(key, 4)
        x = jax.random.normal(k1, (B, N, D_IN), dtype=jnp.float32)
        A_shape = jax.random.uniform(k2, (B, N, N), dtype=jnp.float32)
        w = jax.random.normal(k3, (D_IN, D_OUT), dtype=jnp.float32)
        a = jax.random.normal(k4, (D_OUT,), dtype=jnp.float32)
        return {'x': x, 'A_shape': A_shape, 'w': w, 'a': a}
    _L3_gnn_all = _L3_gnn_setup()
    _L3_gnn_in = {k: v for k, v in _L3_gnn_all.items() if k in ('w', 'a')}
    del _L3_gnn_all
    return {'x': x, 'adj': adj, 'L0_gnn_W1': _L0_gnn_in['W1'], 'L0_gnn_b1': _L0_gnn_in['b1'], 'L0_gnn_gamma': _L0_gnn_in['gamma'], 'L0_gnn_beta': _L0_gnn_in['beta'], 'L0_gnn_W2': _L0_gnn_in['W2'], 'L0_gnn_b2': _L0_gnn_in['b2'], 'L1_gnn_W1': _L1_gnn_in['W1'], 'L1_gnn_b1': _L1_gnn_in['b1'], 'L1_gnn_W2': _L1_gnn_in['W2'], 'L1_gnn_b2': _L1_gnn_in['b2'], 'L1_gnn_W3': _L1_gnn_in['W3'], 'L1_gnn_b3': _L1_gnn_in['b3'], 'L2_gnn_W': _L2_gnn_in['W'], 'L3_gnn_w': _L3_gnn_in['w'], 'L3_gnn_a': _L3_gnn_in['a']}

def reference(x, adj, L0_gnn_W1, L0_gnn_b1, L0_gnn_gamma, L0_gnn_beta, L0_gnn_W2, L0_gnn_b2, L1_gnn_W1, L1_gnn_b1, L1_gnn_W2, L1_gnn_b2, L1_gnn_W3, L1_gnn_b3, L2_gnn_W, L3_gnn_w, L3_gnn_a):
    import jax
    import jax.numpy as jnp

    def _L0_gnn_ref(x, adj, W1, b1, gamma, beta, W2, b2):
        import jax, jax.numpy as jnp
        import numpy as np
        EPS_LN = 1e-05

        def hypergraph_conv(x, adj, W, b):
            N, C, _ = adj.shape
            H = (adj != 0).astype(x.dtype)
            w = adj.reshape(N, -1)[:, :C]
            xw = jnp.einsum('ncd,hd->nch', x, W)
            Dn = jnp.einsum('nce,ne->nc', H, w)
            Dn = jnp.where(Dn > 0, 1.0 / Dn, 0.0)
            Be = H.sum(axis=1)
            Be = jnp.where(Be > 0, 1.0 / Be, 0.0)
            m = Be[:, :, None] * jnp.einsum('nce,nch->neh', H, xw)
            out = Dn[:, :, None] * jnp.einsum('nce,neh->nch', H, m)
            return out + b

        def layer_norm(x, g, b):
            mu = jnp.mean(x, axis=-1, keepdims=True)
            var = jnp.var(x, axis=-1, keepdims=True)
            return (x - mu) * jax.lax.rsqrt(var + EPS_LN) * g + b
        h = jax.nn.relu(hypergraph_conv(x, adj, W1, b1))
        h = layer_norm(h, gamma, beta)
        y = hypergraph_conv(h, adj, W2, b2)
        return y + x

    def _L1_gnn_ref(batch_graph, adj, W1, b1, W2, b2, W3, b3):
        import jax, jax.numpy as jnp
        import numpy as np
        B, N, F_IN, F_HID, F_OUT = (32, 512, 256, 256, 256)

        def _gcn_layer(x, adj, W, b):
            support = jnp.einsum('bnf,fh->bnh', x, W)
            return jnp.einsum('bnm,bmh->bnh', adj, support) + b
        x = jax.nn.relu(_gcn_layer(batch_graph, adj, W1, b1))
        x = jax.nn.relu(_gcn_layer(x, adj, W2, b2))
        out = _gcn_layer(x, adj, W3, b3)
        return out

    def _L2_gnn_ref(x, adj, W):
        import jax, jax.numpy as jnp
        import numpy as np
        EPS = 1e-06
        deg = jnp.sum(adj, axis=-1, keepdims=True)
        agg = jnp.einsum('bij,bjf->bif', adj, x) / jnp.maximum(deg, EPS)
        cat = jnp.concatenate([x, agg], axis=2)
        out = jnp.einsum('bnf,of->bno', cat, W)
        return jax.nn.relu(out)

    def _L3_gnn_ref(x, A_shape, w, a):
        import jax, jax.numpy as jnp
        import numpy as np
        B, N, D_IN, D_OUT = (4, 2048, 256, 256)
        y = x @ w
        s = y @ a
        A = s[..., :, None] + s[..., None, :]
        A = jnp.tanh(A / 8.0) * 8.0
        A = jnp.where(A >= 0, A, 0.1 * A)
        A = jnp.exp(A) * A_shape
        A = A / jnp.sum(A, axis=-1, keepdims=True)
        A = A * jnp.sum(A_shape, axis=-1, keepdims=True)
        out = A @ x @ w
        return out
    x = _layernorm(x + _L0_gnn_ref(x, adj, L0_gnn_W1, L0_gnn_b1, L0_gnn_gamma, L0_gnn_beta, L0_gnn_W2, L0_gnn_b2), axis=-1)
    x = _layernorm(x + _L1_gnn_ref(x, adj, L1_gnn_W1, L1_gnn_b1, L1_gnn_W2, L1_gnn_b2, L1_gnn_W3, L1_gnn_b3), axis=-1)
    x = _layernorm(x + _L2_gnn_ref(x, adj, L2_gnn_W), axis=-1)
    x = _layernorm(x + _L3_gnn_ref(x, adj, L3_gnn_w, L3_gnn_a), axis=-1)
    return x

_drawn_inputs = setup_inputs


def setup_inputs(seed=0):
    import zlib

    import numpy as np

    out = dict(_drawn_inputs(seed))
    spreads = {'L0_gnn_b1': (0.0, 0.1),
     'L0_gnn_gamma': (1.0, 0.2),
     'L0_gnn_beta': (0.0, 0.1),
     'L0_gnn_b2': (0.0, 0.1),
     'L1_gnn_b1': (0.0, 0.8),
     'L1_gnn_b2': (0.0, 0.8),
     'L1_gnn_b3': (0.0, 0.8)}
    factors = {'L3_gnn_a': 8.0}
    for name, (base, spread) in spreads.items():
        noise = np.random.default_rng([zlib.crc32(name.encode()), seed]).standard_normal(out[name].shape)
        drawn = base * np.exp(spread * noise) if base else spread * noise
        out[name] = jnp.asarray(drawn.astype(out[name].dtype))
    for name, factor in factors.items():
        out[name] = (out[name] * factor).astype(out[name].dtype)
    return out
```

```python
from contextlib import ExitStack

import concourse.bass as bass
from concourse import mybir

F32 = mybir.dt.float32
F32R = mybir.dt.float32r
ALU = mybir.AluOpType
ACT = mybir.ActivationFunctionType
AX = mybir.AxisListType

P = 128
LANES = 4
EPS_LN = 1e-5
EPS_DEG = 1e-6
TINY = 1e-38

STAGES = ["load", "adj_transpose", "adj_split", "hyper_scale", "K", "Z", "U", "h_transpose", "P", "y", "ln1",
          "Z1", "X1", "S2", "X2", "S3", "o3", "ln2", "x2_transpose", "S", "agg", "ln3",
          "x3_transpose", "Y", "scores", "attn", "R", "ln4"]
PE = ["adjT", "d", "K", "Z", "U0", "U1", "hT", "P", "y", "Z1", "X1", "S2", "X2", "S3", "o3",
      "x2T", "S", "P1", "agg", "x3T", "Y", "s_row", "R"]
SC = ["aT", "Kh", "Zh", "h", "hTh", "Vh", "Z1h", "X1h", "S2h", "X2h", "S3h", "x2Th", "Sh", "P1", "x3Th",
      "Yh", "tanh", "exp", "Ah"]
DV = ["xh", "xl", "xa", "aTh", "HT", "cnt", "Be", "Beh", "Bel", "BHl", "dmax", "drec", "Dn", "Kl", "Zl", "Upre", "bnh",
      "aggrh", "hTl", "V", "t1", "bn1", "aggr1", "x1", "x1h", "Z1l", "X1l", "S2l", "X2l", "S3l", "t2",
      "bn2", "aggr2", "x2", "x2Tl", "Sl", "deg", "rdeg", "u", "t3", "bn3", "aggr3", "x3", "x3Tl",
      "s8", "Yl", "leaky", "Al", "rrec", "q", "t4", "bn4", "aggr4", "out"]
GP = ["aTl", "BHh", "epsh", "rsh", "Vl", "eps1", "rs1", "x1l", "x1b", "eps2", "rs2", "eps3", "rs3", "A",
      "eps4", "rs4"]


class Round:

    def __init__(self, eng, index, behind=0, bases=None, scratch=None):
        self.eng, self.index, self.behind, self.bases, self.scratch = eng, index, behind, bases, scratch
        self.number = None if bases else index - behind
        self.first = self.number == 0
        self.graph = index - behind

    def last(self):
        return Round(self.eng, self.index, self.behind + 1, self.bases, self.scratch)

    def count(self, each, plus):
        if self.bases is None:
            return self.number * each + plus
        if plus == self.behind * each:
            return self.bases[each]
        self.eng.reg_add(self.scratch, self.bases[each], plus - self.behind * each)
        return self.scratch


def done(steps, name, it):
    return it.count(len(steps), steps.index(name) + 1)


def graph_layers(nc, x, adj, W1T, b1, gamma, beta, W2T, b2, C1, c1, C2, c2, C3, c3, WT, w, a, out):
    GRAPHS, N, F = x.shape
    FH = W1T.shape[1]
    T = N // P
    TH = FH // P
    ROUNDS = GRAPHS // LANES
    assert N == F == T * P and GRAPHS == ROUNDS * LANES
    SHIFT = [len(STAGES) * q // LANES for q in range(LANES)]

    with ExitStack() as ctx:
        def sb(name, shape, dt=F32):
            return ctx.enter_context(nc.sbuf_tensor(name, shape, dt))

        def sem(name):
            return ctx.enter_context(nc.semaphore(name))

        def per_lane(make):
            return [make(q) for q in range(LANES)]

        def pair(name, shape):
            return sb(name + "_high", shape, F32R), sb(name + "_low", shape, F32R)

        a_buf = per_lane(lambda q: sb(f"adj{q}", [P, T, N]))
        cur = per_lane(lambda q: sb(f"cur{q}", [P, T, F]))
        tmp = per_lane(lambda q: sb(f"tmp{q}", [P, T, F]))
        aT = per_lane(lambda q: pair(f"aT{q}", [P, T, N]))
        K = per_lane(lambda q: pair(f"K{q}", [P, T, N]))
        op = per_lane(lambda q: pair(f"op{q}", [P, T, N]))
        rows = per_lane(lambda q: pair(f"rows{q}", [P, T, F + 2]))
        hid = per_lane(lambda q: sb(f"hid{q}", [P, 2 * T, F]))
        big = per_lane(lambda q: pair(f"big{q}", [P, TH, N]))
        small = per_lane(lambda q: sb(f"small{q}", [P, 64]))
        bc = per_lane(lambda q: pair(f"inv_count{q}", [P, T]))
        ps = per_lane(lambda q: ctx.enter_context(nc.psum_tensor(f"ps{q}", [P, 2, 512], F32)))

        W1p = pair("W1T", [P, T, FH])
        W2p = pair("W2T", [P, TH, F])
        Cp = [pair(f"C{n}", [P, T, F]) for n in (1, 2, 3)]
        WTp = pair("WT", [P, 2 * T, F])
        wp = pair("w3", [P, T, F + 2])
        b1_t = sb("b1_t", [P, FH])
        bb_t = sb("bb_t", [P, F])
        b2_t = sb("b2_t", [P, F])
        c3_t = sb("c3_t", [P, F])
        ident = sb("ident", [P, P])
        ones = sb("ones", [P, P])
        ones_row = sb("ones_row", [2, N], F32R)
        c_raw = sb("c_raw", [2, 2 * F])
        c_high = sb("c_high", [2, 2 * F], F32R)
        c_mid = sb("c_mid", [2, 2 * F])
        c_row = sb("c_row", [2, 2 * F], F32R)
        pick = sb("pick", [2, 2])
        minus_half = sb("minus_half", [P, T])
        eps_col = sb("eps_col", [P, T])
        gam = sb("gam", [P, TH])
        bet = sb("bet", [P, TH])
        vcol = sb("vcol", [P, T])

        pe_done = per_lane(lambda q: sem(f"pe_done{q}"))
        sc_done = per_lane(lambda q: sem(f"sc_done{q}"))
        dv_done = per_lane(lambda q: sem(f"dv_done{q}"))
        gp_done = per_lane(lambda q: sem(f"gp_done{q}"))
        adj_in = per_lane(lambda q: sem(f"adj_in{q}"))
        x_in = per_lane(lambda q: sem(f"x_in{q}"))
        stored = per_lane(lambda q: sem(f"stored{q}"))
        w_in = sem("w_in")
        const_set = sem("const_set")
        w_high = sem("w_high")
        w_dve = sem("w_dve")
        w_pe = sem("w_pe")
        w_dve_own = sem("w_dve_own")
        dv_own = per_lane(lambda q: sem(f"dv_own{q}"))

        def st(q):
            return small[q][:, 0:12].rearrange("p (t s) -> p t s", t=T)

        def mv(q):
            return small[q][:, 12:16].rearrange("p (t s) -> p t s", t=T)

        def col(q, n):
            return small[q][:, 16 + 2 * n:18 + 2 * n]
        VE, RS, CNT, CMAX, BE, DMAX, DREC, DN, DEG, DEGC, RDEG, RREC, QQ, S8 = range(14)

        def f32(t):
            return t.bitcast(F32)

        HT = [big[q][0][:, 0:T, :] for q in range(LANES)]
        BH = [(big[q][0][:, T:2 * T, :], big[q][1][:, 0:T, :]) for q in range(LANES)]
        AP_ = [(big[q][0][:, 0:T, :], big[q][1][:, 0:T, :]) for q in range(LANES)]
        E_ = [hid[q][:, 0:T, :] for q in range(LANES)]
        A_ = [hid[q][:, T:2 * T, :] for q in range(LANES)]
        h512 = [hid[q][:, :, :].rearrange("p (t u) f -> p t (u f)", t=T) for q in range(LANES)]
        bank = [[ps[q][:, b, :].rearrange("p (t f) -> p t f", t=T) for b in range(2)] for q in range(LANES)]

        raw = {"W1": h512[0], "W2": hid[1][:, :, :], "WT": hid[2][:, :, :], "C0": tmp[0][:, :, :],
               "C1": tmp[1][:, :, :], "C2": tmp[2][:, :, :], "w": tmp[3][:, :, :], "a": hid[3][:, 0, :],
               "prod": hid[3][:, 1, :]}

        def rounds(eng, name, stage_of):
            def a_pass(i, first, last, bases, scratch):
                for slot in range(len(STAGES)):
                    for q in range(LANES):
                        late = slot < SHIFT[q]
                        if (first and late) or (last and not late):
                            continue
                        step = stage_of.get(STAGES[(slot - SHIFT[q]) % len(STAGES)])
                        if step:
                            step(q, Round(eng, i, int(late), bases, scratch))
            a_pass(0, True, False, None, None)
            scratch = eng.alloc_register(f"{name}_value")
            kinds = sorted({len(PE), len(SC), len(DV), len(GP), 16, 1})
            bases = {each: eng.alloc_register(f"{name}_rounds_x{each}") for each in kinds}
            for each in kinds:
                eng.reg_mov(bases[each], each)
            with eng.Fori(1, ROUNDS) as i:
                a_pass(i, False, False, bases, scratch)
                for each in kinds:
                    eng.reg_add(bases[each], bases[each], each)
            a_pass(ROUNDS, False, True, None, None)

        W_DONE = 13
        block = ctx.enter_context(nc.Block())

        @block.sync
        def _(sp):
            def tiles(w_, t):
                return w_.rearrange("(t p) f -> p t f", t=t)

            def over_rows(v, n):
                return v.rearrange("(a n) -> a n", a=1).to_broadcast([P, n])
            for dst, src in ((raw["W1"], tiles(W1T, T)), (raw["W2"], tiles(W2T, TH)), (raw["WT"], tiles(WT, 2 * T)),
                             (raw["C0"], tiles(C1, T)), (raw["C1"], tiles(C2, T)), (raw["C2"], tiles(C3, T)),
                             (raw["w"], tiles(w, T)),
                             (raw["a"], over_rows(a, F)), (b1_t[:, :], over_rows(b1, FH)),
                             (b2_t[:, :], over_rows(b2, F)), (c3_t[:, :], over_rows(c3, F)),
                             (gam[:, :], gamma), (bet[:, :], beta)):
                sp.dma_start(dst, src).then_inc(w_in, 16)
            for n, c in enumerate((c1, c2)):
                for r in range(2):
                    sp.dma_start(c_raw[r:r + 1, n * F:(n + 1) * F],
                                 c.rearrange("(a n) -> a n", a=1)).then_inc(w_in, 16)

            def load(q, it):
                g = it.graph * LANES + q
                if it.first:
                    sp.wait_ge(w_dve, W_DONE)
                else:
                    sp.wait_ge(gp_done[q], done(GP, "A", it.last()))
                sp.dma_start(a_buf[q][:, :, :],
                             adj[bass.ds(g, 1), :, :].rearrange("g (t p) n -> p (g t) n", p=P)).then_inc(adj_in[q], 16)
                if not it.first:
                    sp.wait_ge(dv_done[q], done(DV, "t4", it.last()))
                sp.dma_start(cur[q][:, :, :],
                             x[bass.ds(g, 1), :, :].rearrange("g (t p) n -> p (g t) n", p=P)).then_inc(x_in[q], 16)

            def store(q, it):
                g = it.graph * LANES + q
                sp.wait_ge(dv_done[q], done(DV, "out", it))
                sp.dma_start(out[bass.ds(g, 1), :, :].rearrange("g (t p) n -> p (g t) n", p=P),
                             hid[q][:, 0:T, :]).then_inc(stored[q], 16)

            rounds(sp, "sp", {"load": load, "ln4": store})
            for q in range(LANES):
                sp.wait_ge(stored[q], 16 * ROUNDS)

        @block.tensor
        def _(pe):
            def product(dst, left, right, contract, cols, bias=None, two=False):
                passes = [(1, 0), (0, 0)] if two else [(1, 0), (0, 1), (0, 0)]
                for m, d in enumerate(dst):
                    if bias is not None:
                        nc.tensor.matmul(d, c_row[:, bias + m * P:bias + (m + 1) * P], ones_row[:, :],
                                         start=True, stop=False)
                    for n, (i, j) in enumerate(passes):
                        for k in range(contract):
                            last = nc.tensor.matmul(d, left[i][:, k, m * P:(m + 1) * P], right[j][:, k, 0:cols],
                                                    start=(bias is None and n == 0 and k == 0),
                                                    stop=(n == len(passes) - 1 and k == contract - 1))
                return last

            pe.wait_ge(const_set, 2)
            pe.wait_ge(w_dve, 2)
            for k in range(TH):
                nc.tensor.matmul(ps[0][:, 0, 0:F], ones[:, :], hid[0][:, k, :], start=(k == 0), stop=(k == TH - 1))
            for k in range(TH):
                last = nc.tensor.matmul(ps[0][:, 1, 0:F], bet[:, k:k + 1].to_broadcast([P, P]), raw["W2"][:, k, :],
                                        start=(k == 0), stop=(k == TH - 1))
            last.then_inc(w_pe, 1)
            pe.wait_ge(w_dve, W_DONE)
            pe.wait_ge(w_high, 6)

            def banks(q):
                return [ps[q][:, b, 0:F + 2] for b in range(2)]

            def tiles(q, b=0):
                return [bank[q][b][:, t, :] for t in range(T)]

            def adj_transpose(q, it):
                pe.wait_ge(adj_in[q], it.count(16, 16))
                if not it.first:
                    pe.wait_ge(dv_done[q], done(DV, "t4", it.last()))
                for t in range(T):
                    for u in range(T):
                        last = nc.tensor.transpose(bank[q][0][:, t, u * P:(u + 1) * P],
                                                   a_buf[q][:, u, t * P:(t + 1) * P], ident[:, :])
                last.then_inc(pe_done[q], 1)

            def k_product(q, it):
                pe.wait_ge(gp_done[q], done(GP, "aTl", it))
                pe.wait_ge(dv_done[q], done(DV, "HT", it))
                for t in range(T):
                    for n in range(2):
                        for k in range(T):
                            last = nc.tensor.matmul(ps[q][:, 1, 2 * t:2 * t + 2], HT[q][:, k, t * P:(t + 1) * P],
                                                    aT[q][1 - n][:, k, 0:2], start=(n == 0 and k == 0),
                                                    stop=(n == 1 and k == T - 1))
                last.then_inc(pe_done[q], 1)
                pe.wait_ge(gp_done[q], done(GP, "BHh", it))
                pe.wait_ge(dv_done[q], done(DV, "BHl", it))
                pe.wait_ge(sc_done[q], done(SC, "aT", it))
                product(tiles(q), BH[q], (HT[q],), T, N, two=True).then_inc(pe_done[q], 1)

            def z_product(q, it):
                pe.wait_ge(sc_done[q], done(SC, "Kh", it))
                pe.wait_ge(dv_done[q], done(DV, "Kl", it))
                product(tiles(q), rows[q], K[q], T, N).then_inc(pe_done[q], 1)

            def u_product(q, it):
                pe.wait_ge(sc_done[q], done(SC, "Zh", it))
                pe.wait_ge(dv_done[q], done(DV, "Zl", it))
                for m in range(T):
                    left = [v[:, :, m * P:(m + 1) * P] for v in op[q]]
                    product([ps[q][:, m, :]], left, W1p, T, FH).then_inc(pe_done[q], 1)

            def h_transpose(q, it):
                pe.wait_ge(sc_done[q], done(SC, "h", it))
                for f in range(TH):
                    for t in range(T):
                        last = nc.tensor.transpose(bank[q][f // 2][:, f % 2, t * P:(t + 1) * P],
                                                   h512[q][:, t, f * P:(f + 1) * P], ident[:, :])
                last.then_inc(pe_done[q], 1)

            def p_product(q, it):
                pe.wait_ge(sc_done[q], done(SC, "hTh", it))
                pe.wait_ge(dv_done[q], done(DV, "hTl", it))
                product(tiles(q), big[q], W2p, TH, F).then_inc(pe_done[q], 1)

            def y_product(q, it):
                pe.wait_ge(sc_done[q], done(SC, "Vh", it))
                pe.wait_ge(gp_done[q], done(GP, "Vl", it))
                product(tiles(q), K[q], op[q], T, F).then_inc(pe_done[q], 1)

            def z1_product(q, it):
                pe.wait_ge(dv_done[q], done(DV, "x1h", it))
                pe.wait_ge(gp_done[q], done(GP, "x1l", it))
                product(tiles(q), rows[q], aT[q], T, N).then_inc(pe_done[q], 1)

            def x1_product(q, it):
                pe.wait_ge(sc_done[q], done(SC, "Z1h", it))
                pe.wait_ge(dv_done[q], done(DV, "Z1l", it))
                product(tiles(q), Cp[0], op[q], T, N, bias=0).then_inc(pe_done[q], 1)

            def s2_product(q, it):
                pe.wait_ge(sc_done[q], done(SC, "X1h", it))
                pe.wait_ge(dv_done[q], done(DV, "X1l", it))
                product(tiles(q), op[q], Cp[1], T, F).then_inc(pe_done[q], 1)

            def x2_product(q, it):
                pe.wait_ge(sc_done[q], done(SC, "S2h", it))
                pe.wait_ge(dv_done[q], done(DV, "S2l", it))
                product(tiles(q), op[q], aT[q], T, N, bias=F).then_inc(pe_done[q], 1)

            def s3_product(q, it):
                pe.wait_ge(sc_done[q], done(SC, "X2h", it))
                pe.wait_ge(dv_done[q], done(DV, "X2l", it))
                product(tiles(q), op[q], Cp[2], T, F).then_inc(pe_done[q], 1)

            def o3_product(q, it):
                pe.wait_ge(sc_done[q], done(SC, "S3h", it))
                pe.wait_ge(dv_done[q], done(DV, "S3l", it))
                product(tiles(q), aT[q], op[q], T, F).then_inc(pe_done[q], 1)

            def cur_transpose(q):
                for f in range(T):
                    for t in range(T):
                        last = nc.tensor.transpose(bank[q][0][:, f, t * P:(t + 1) * P],
                                                   cur[q][:, t, f * P:(f + 1) * P], ident[:, :])
                last.then_inc(pe_done[q], 1)

            def x2_transpose(q, it):
                pe.wait_ge(dv_done[q], done(DV, "x2", it))
                cur_transpose(q)

            def s_product(q, it):
                pe.wait_ge(sc_done[q], done(SC, "x2Th", it))
                pe.wait_ge(dv_done[q], done(DV, "x2Tl", it))
                product(tiles(q), op[q], [v[:, T:2 * T, :] for v in WTp], T, F).then_inc(pe_done[q], 1)
                product(tiles(q, 1), op[q], [v[:, 0:T, :] for v in WTp], T, F).then_inc(pe_done[q], 1)

            def agg_product(q, it):
                pe.wait_ge(sc_done[q], done(SC, "P1", it))
                pe.wait_ge(dv_done[q], done(DV, "Sl", it))
                product(banks(q), aT[q], rows[q], T, F + 2).then_inc(pe_done[q], 1)

            def x3_transpose(q, it):
                pe.wait_ge(dv_done[q], done(DV, "x3", it))
                cur_transpose(q)

            def y3_product(q, it):
                pe.wait_ge(sc_done[q], done(SC, "x3Th", it))
                pe.wait_ge(dv_done[q], done(DV, "x3Tl", it))
                product(banks(q), op[q], wp, T, F + 2).then_inc(pe_done[q], 1)

            def s_row(q, it):
                pe.wait_ge(dv_done[q], done(DV, "Yl", it))
                for t in range(T):
                    last = nc.tensor.transpose(bank[q][0][:, 0, t * P:(t + 1) * P],
                                               col(q, S8)[:, t:t + 1].to_broadcast([P, P]), ident[:, :])
                last.then_inc(pe_done[q], 1)

            def r_product(q, it):
                pe.wait_ge(sc_done[q], done(SC, "Ah", it))
                pe.wait_ge(dv_done[q], done(DV, "Al", it))
                product(banks(q), AP_[q], rows[q], T, F + 2).then_inc(pe_done[q], 1)

            rounds(pe, "pe", {"adj_transpose": adj_transpose, "K": k_product, "Z": z_product, "U": u_product,
                        "h_transpose": h_transpose, "P": p_product, "y": y_product, "Z1": z1_product,
                        "X1": x1_product, "S2": s2_product, "X2": x2_product, "S3": s3_product, "o3": o3_product,
                        "x2_transpose": x2_transpose, "S": s_product, "agg": agg_product,
                        "x3_transpose": x3_transpose, "Y": y3_product, "scores": s_row, "R": r_product})

        @block.scalar
        def _(act):
            act.wait_ge(w_in, 16 * 17)
            for v, src in ((W1p, raw["W1"]), (WTp, raw["WT"]), (Cp[0], raw["C0"]), (Cp[1], raw["C1"]),
                           (Cp[2], raw["C2"])):
                nc.scalar.activation(v[0][:, :, :], src, ACT.Copy).then_inc(w_high, 1)
            nc.scalar.activation(wp[0][:, :, 0:F], raw["w"], ACT.Copy).then_inc(w_high, 1)

            def adj_copy(q, it):
                act.wait_ge(pe_done[q], done(PE, "adjT", it))
                nc.scalar.activation(a_buf[q][:, :, :], bank[q][0], ACT.Copy).then_inc(sc_done[q], 1)

            def k_high(q, it):
                act.wait_ge(pe_done[q], done(PE, "K", it))
                nc.scalar.activation(K[q][0][:, :, :], bank[q][0], ACT.Copy).then_inc(sc_done[q], 1)

            def evacuate(name, func=ACT.Copy):
                def step(q, it):
                    act.wait_ge(pe_done[q], done(PE, name, it))
                    nc.scalar.activation(op[q][0][:, :, :], bank[q][0], func).then_inc(sc_done[q], 1)
                return step

            def hidden_relu(q, it):
                act.wait_ge(dv_done[q], done(DV, "Upre", it))
                nc.scalar.activation(hid[q][:, :, :], hid[q][:, :, :], ACT.Relu).then_inc(sc_done[q], 1)

            def hidden_high(q, it):
                act.wait_ge(pe_done[q], done(PE, "hT", it))
                nc.scalar.activation(big[q][0][:, :, :], ps[q][:, :, :].rearrange("p b (t n) -> p (b t) n", t=T), ACT.Copy).then_inc(sc_done[q], 1)

            def v_high(q, it):
                act.wait_ge(dv_done[q], done(DV, "V", it))
                nc.scalar.activation(op[q][0][:, :, :], hid[q][:, 0:T, :], ACT.Copy).then_inc(sc_done[q], 1)

            def s_high(q, it):
                act.wait_ge(pe_done[q], done(PE, "S", it))
                nc.scalar.activation(rows[q][0][:, :, 0:F], bank[q][0], ACT.Copy).then_inc(sc_done[q], 1)
                act.wait_ge(pe_done[q], done(PE, "P1", it))
                nc.scalar.activation(hid[q][:, 0:T, :], bank[q][1], ACT.Copy).then_inc(sc_done[q], 1)

            def y3_high(q, it):
                act.wait_ge(pe_done[q], done(PE, "Y", it))
                nc.scalar.activation(rows[q][0][:, :, 0:F], ps[q][:, :, 0:F], ACT.Copy).then_inc(sc_done[q], 1)

            def scores(q, it):
                act.wait_ge(pe_done[q], done(PE, "s_row", it))
                for t in range(T):
                    last = nc.scalar.activation(tmp[q][:, t, :], ps[q][:, 0, 0:N], ACT.Tanh, bias=col(q, S8)[:, t:t + 1])
                last.then_inc(sc_done[q], 1)
                act.wait_ge(dv_done[q], done(DV, "leaky", it))
                nc.scalar.activation(E_[q], tmp[q][:, :, :], ACT.Exp, scale=8.0).then_inc(sc_done[q], 1)

            def a_high(q, it):
                act.wait_ge(gp_done[q], done(GP, "A", it))
                nc.scalar.activation(AP_[q][0], A_[q], ACT.Copy).then_inc(sc_done[q], 1)

            rounds(act, "act", {"adj_transpose": adj_copy, "K": k_high, "Z": evacuate("Z"), "U": hidden_relu,
                         "h_transpose": hidden_high, "P": v_high, "Z1": evacuate("Z1"), "X1": evacuate("X1", ACT.Relu),
                         "S2": evacuate("S2"), "X2": evacuate("X2", ACT.Relu), "S3": evacuate("S3"),
                         "x2_transpose": evacuate("x2T"), "S": s_high, "x3_transpose": evacuate("x3T"),
                         "Y": y3_high, "scores": scores, "attn": a_high})

        @block.vector
        def _(dve):
            dve.wait_ge(w_in, 16 * 17)
            dve.wait_ge(w_high, 1)
            nc.vector.tensor_tensor(W1p[1][:, :, :], raw["W1"], f32(W1p[0][:, :, :]), ALU.subtract).then_inc(w_dve, 1)
            dve.wait_ge(w_dve, 1)
            for k in range(TH):
                last = nc.vector.tensor_scalar(hid[0][:, k, :], raw["W2"][:, k, :], gam[:, k:k + 1], None, ALU.mult)
            last.then_inc(w_dve, 1)
            dve.wait_ge(w_high, 6)
            for v, src in ((WTp, raw["WT"]), (Cp[0], raw["C0"]), (Cp[1], raw["C1"]), (Cp[2], raw["C2"])):
                last = nc.vector.tensor_tensor(v[1][:, :, :], src, f32(v[0][:, :, :]), ALU.subtract)
            nc.vector.tensor_tensor(wp[1][:, :, 0:F], raw["w"], f32(wp[0][:, :, 0:F]), ALU.subtract).then_inc(w_dve, 1)
            for k in range(T):
                nc.vector.tensor_tensor(hid[3][:, 1 + k, :], raw["w"][:, k, :], raw["a"], ALU.mult).then_inc(w_dve, 1)
            dve.wait_ge(w_dve, 5)
            nc.vector.reduce_sum(vcol[:, :], hid[3][:, 1:1 + T, :], AX.X).then_inc(w_dve, 1)
            dve.wait_ge(w_dve, 6)
            dve.wait_ge(const_set, 3)
            nc.vector.tensor_copy(wp[0][:, :, F:F + 1], vcol[:, :].unsqueeze(2)).then_inc(w_dve, 1)
            dve.wait_ge(w_dve, 7)
            nc.vector.tensor_tensor(wp[1][:, :, F:F + 1], vcol[:, :].unsqueeze(2), f32(wp[0][:, :, F:F + 1]),
                                    ALU.subtract).then_inc(w_dve, 1)
            nc.vector.tensor_copy(c_high[:, :], c_raw[:, :]).then_inc(w_dve, 1)
            dve.wait_ge(w_dve, 9)
            nc.vector.tensor_scalar(c_mid[:, :], f32(c_high[:, :]), pick[:, 1:2], None, ALU.mult).then_inc(w_dve, 1)
            dve.wait_ge(w_dve, 10)
            nc.vector.scalar_tensor_tensor(c_row[:, :], c_raw[:, :], pick[:, 0:1], c_mid[:, :], ALU.mult,
                                           ALU.add).then_inc(w_dve, 1)
            dve.wait_ge(w_pe, 1)
            nc.vector.tensor_copy(bb_t[:, :], ps[0][:, 1, 0:F])
            for k in range(TH):
                last = nc.vector.scalar_tensor_tensor(hid[1][:, k, :], ps[0][:, 0, 0:F], -1.0 / FH, hid[0][:, k, :],
                                                      ALU.mult, ALU.add)
            last.then_inc(w_dve, 1)
            dve.wait_ge(w_dve, 12)
            nc.vector.tensor_copy(W2p[0][:, :, :], hid[1][:, :, :]).then_inc(w_dve_own, 1)
            dve.wait_ge(w_dve_own, 1)
            nc.vector.tensor_tensor(W2p[1][:, :, :], hid[1][:, :, :], f32(W2p[0][:, :, :]),
                                    ALU.subtract).then_inc(w_dve, 1)
            dve.wait_ge(w_dve, W_DONE)

            def own(q, name, it):
                dve.wait_ge(dv_done[q], done(DV, name, it))

            def x_split(q, it):
                dve.wait_ge(x_in[q], it.count(16, 16))
                if not it.first:
                    dve.wait_ge(pe_done[q], done(PE, "R", it.last()))
                nc.vector.tensor_copy(rows[q][0][:, :, 0:F], cur[q][:, :, :]).then_inc(dv_done[q], 1)
                own(q, "xh", it)
                nc.vector.tensor_tensor(rows[q][1][:, :, 0:F], cur[q][:, :, :], f32(rows[q][0][:, :, 0:F]),
                                        ALU.subtract).then_inc(dv_done[q], 1)
                own(q, "xl", it)
                for t in range(T):
                    last = nc.vector.scalar_tensor_tensor(cur[q][:, t, :], cur[q][:, t, :], 2.0, b2_t[:, :],
                                                          ALU.mult, ALU.add)
                last.then_inc(dv_done[q], 1)

            def adj_split(q, it):
                dve.wait_ge(sc_done[q], done(SC, "aT", it))
                nc.vector.tensor_copy(aT[q][0][:, :, :], a_buf[q][:, :, :]).then_inc(dv_done[q], 1)
                for k in range(T):
                    last = nc.vector.tensor_scalar(HT[q][:, k, :], a_buf[q][:, k, :], 0.0, 0.0, ALU.not_equal,
                                                   ALU.add, accum_out=col(q, CNT)[:, k:k + 1])
                last.then_inc(dv_done[q], 1)
                own(q, "HT", it)
                nc.vector.tensor_scalar(col(q, CMAX), col(q, CNT), 1.0, None, ALU.max).then_inc(dv_done[q], 1)
                own(q, "cnt", it)
                nc.vector.reciprocal(col(q, BE), col(q, CMAX)).then_inc(dv_done[q], 1)
                own(q, "Be", it)
                nc.vector.tensor_copy(bc[q][0][:, :], col(q, BE)).then_inc(dv_done[q], 1)
                own(q, "Beh", it)
                nc.vector.tensor_tensor(bc[q][1][:, :], col(q, BE), f32(bc[q][0][:, :]), ALU.subtract).then_inc(dv_done[q], 1)
                own(q, "Bel", it)
                nc.vector.tensor_tensor(BH[q][1], f32(HT[q]), f32(bc[q][1][:, :]).unsqueeze(2).to_broadcast([P, T, N]),
                                        ALU.mult).then_inc(dv_done[q], 1)

            def k_low(q, it):
                dve.wait_ge(pe_done[q], done(PE, "d", it))
                d = ps[q][:, 1, 0:2 * T:2]
                nc.vector.tensor_scalar(col(q, DMAX), d, TINY, None, ALU.max).then_inc(dv_done[q], 1)
                own(q, "dmax", it)
                nc.vector.reciprocal(col(q, DREC), col(q, DMAX)).then_inc(dv_done[q], 1)
                own(q, "drec", it)
                nc.vector.scalar_tensor_tensor(col(q, DN), d, 0.0, col(q, DREC), ALU.is_gt, ALU.mult).then_inc(dv_done[q], 1)
                dve.wait_ge(sc_done[q], done(SC, "Kh", it))
                nc.vector.tensor_tensor(K[q][1][:, :, :], bank[q][0], f32(K[q][0][:, :, :]), ALU.subtract).then_inc(dv_done[q], 1)

            def evacuate(high):
                def step(q, it):
                    dve.wait_ge(sc_done[q], done(SC, high, it))
                    nc.vector.tensor_tensor(op[q][1][:, :, :], bank[q][0], f32(op[q][0][:, :, :]),
                                            ALU.subtract).then_inc(dv_done[q], 1)
                return step

            def evacuate_relu(high):
                def step(q, it):
                    dve.wait_ge(sc_done[q], done(SC, high, it))
                    nc.vector.scalar_tensor_tensor(op[q][1][:, :, :], bank[q][0], 0.0, f32(op[q][0][:, :, :]),
                                                   ALU.max, ALU.subtract).then_inc(dv_done[q], 1)
                return step

            def hidden(q, it):
                if not it.first:
                    dve.wait_ge(stored[q], it.count(16, 0))
                for t in range(T):
                    dve.wait_ge(pe_done[q], done(PE, f"U{t}", it))
                    last = nc.vector.scalar_tensor_tensor(h512[q][:, t, :], ps[q][:, t, :], col(q, DN)[:, t:t + 1],
                                                          b1_t[:, :], ALU.mult, ALU.add)
                last.then_inc(dv_done[q], 1)
                dve.wait_ge(sc_done[q], done(SC, "h", it))
                for t in range(T):
                    last = nc.vector.bn_stats(st(q)[:, t, :], h512[q][:, t, :])
                last.then_inc(dv_done[q], 1)
                aggregate(q, it, "bnh")

            def aggregate(q, it, stats):
                own(q, stats, it)
                nc.vector.tensor_copy(small[q][:, 60:61], st(q)[:, 0, 0:1])
                for t in range(T):
                    last = nc.vector.bn_aggr(mv(q)[:, t, :], st(q)[:, t, :])
                last.then_inc(dv_done[q], 1)

            def statistics(q, it, before, stats):
                own(q, before, it)
                for t in range(T):
                    last = nc.vector.bn_stats(st(q)[:, t, :], tmp[q][:, t, :])
                last.then_inc(dv_done[q], 1)
                aggregate(q, it, stats)

            def normalise(q, it, dst, root):
                dve.wait_ge(gp_done[q], done(GP, root, it))
                for t in range(T):
                    last = nc.vector.tensor_scalar(dst[:, t, :], tmp[q][:, t, :], mv(q)[:, t, 0:1],
                                                   col(q, RS)[:, t:t + 1], ALU.subtract, ALU.mult)
                last.then_inc(dv_done[q], 1)

            def hidden_low(q, it):
                dve.wait_ge(sc_done[q], done(SC, "hTh", it))
                nc.vector.tensor_tensor(big[q][1][:, :, :], ps[q][:, :, :].rearrange("p b (t n) -> p (b t) n", t=T),
                                        f32(big[q][0][:, :, :]), ALU.subtract).then_inc(dv_done[q], 1)

            def v_rows(q, it):
                dve.wait_ge(pe_done[q], done(PE, "P", it))
                dve.wait_ge(gp_done[q], done(GP, "rsh", it))
                for t in range(T):
                    last = nc.vector.scalar_tensor_tensor(hid[q][:, t, :], bank[q][0][:, t, :], col(q, RS)[:, t:t + 1],
                                                          bb_t[:, :], ALU.mult, ALU.add)
                last.then_inc(dv_done[q], 1)

            def t1(q, it):
                dve.wait_ge(pe_done[q], done(PE, "y", it))
                for t in range(T):
                    last = nc.vector.scalar_tensor_tensor(tmp[q][:, t, :], bank[q][0][:, t, :], col(q, DN)[:, t:t + 1],
                                                          cur[q][:, t, :], ALU.mult, ALU.add)
                last.then_inc(dv_done[q], 1)
                statistics(q, it, "t1", "bn1")

            def ln1(q, it):
                normalise(q, it, cur[q], "rs1")
                own(q, "x1", it)
                nc.vector.tensor_copy(rows[q][0][:, :, 0:F], cur[q][:, :, :]).then_inc(dv_done[q], 1)

            def t2(q, it):
                dve.wait_ge(pe_done[q], done(PE, "o3", it))
                dve.wait_ge(gp_done[q], done(GP, "x1b", it))
                nc.vector.tensor_tensor(tmp[q][:, :, :], bank[q][0], tmp[q][:, :, :], ALU.add).then_inc(dv_done[q], 1)
                statistics(q, it, "t2", "bn2")

            def ln2(q, it):
                normalise(q, it, cur[q], "rs2")

            def s_low(q, it):
                dve.wait_ge(sc_done[q], done(SC, "Sh", it))
                nc.vector.tensor_tensor(rows[q][1][:, :, 0:F], bank[q][0], f32(rows[q][0][:, :, 0:F]),
                                        ALU.subtract).then_inc(dv_done[q], 1)

            def t3(q, it):
                dve.wait_ge(pe_done[q], done(PE, "agg", it))
                nc.vector.tensor_copy(col(q, DEG), ps[q][:, :, F]).then_inc(dv_done[q], 1)
                own(q, "deg", it)
                nc.vector.tensor_scalar(col(q, DEGC), col(q, DEG), EPS_DEG, None, ALU.max).then_inc(dv_own[q], 1)
                dve.wait_ge(dv_own[q], it.count(1, 1))
                nc.vector.reciprocal(col(q, RDEG), col(q, DEGC)).then_inc(dv_done[q], 1)
                own(q, "rdeg", it)
                for t in range(T):
                    last = nc.vector.scalar_tensor_tensor(hid[q][:, T + t, :], ps[q][:, t, 0:F], col(q, RDEG)[:, t:t + 1],
                                                          hid[q][:, t, :], ALU.mult, ALU.add)
                last.then_inc(dv_done[q], 1)
                own(q, "u", it)
                nc.vector.scalar_tensor_tensor(tmp[q][:, :, :], hid[q][:, T:2 * T, :], 0.0, cur[q][:, :, :],
                                               ALU.max, ALU.add).then_inc(dv_done[q], 1)
                statistics(q, it, "t3", "bn3")

            def ln3(q, it):
                normalise(q, it, cur[q], "rs3")

            def y3_low(q, it):
                dve.wait_ge(sc_done[q], done(SC, "Yh", it))
                nc.vector.tensor_scalar(col(q, S8), ps[q][:, :, F], 0.125, None, ALU.mult).then_inc(dv_done[q], 1)
                nc.vector.tensor_tensor(rows[q][1][:, :, 0:F], ps[q][:, :, 0:F], f32(rows[q][0][:, :, 0:F]),
                                        ALU.subtract).then_inc(dv_done[q], 1)

            def leaky(q, it):
                dve.wait_ge(sc_done[q], done(SC, "tanh", it))
                nc.vector.scalar_tensor_tensor(tmp[q][:, :, :], tmp[q][:, :, :], 0.1, tmp[q][:, :, :], ALU.mult,
                                               ALU.max).then_inc(dv_done[q], 1)

            def a_low(q, it):
                dve.wait_ge(sc_done[q], done(SC, "Ah", it))
                nc.vector.tensor_tensor(AP_[q][1], A_[q], f32(AP_[q][0]), ALU.subtract).then_inc(dv_done[q], 1)

            def t4(q, it):
                dve.wait_ge(pe_done[q], done(PE, "R", it))
                nc.vector.reciprocal(col(q, RREC), ps[q][:, :, F]).then_inc(dv_done[q], 1)
                own(q, "rrec", it)
                nc.vector.tensor_tensor(col(q, QQ), col(q, RREC), col(q, DEG), ALU.mult).then_inc(dv_done[q], 1)
                own(q, "q", it)
                for t in range(T):
                    last = nc.vector.scalar_tensor_tensor(tmp[q][:, t, :], ps[q][:, t, 0:F], col(q, QQ)[:, t:t + 1],
                                                          cur[q][:, t, :], ALU.mult, ALU.add)
                last.then_inc(dv_done[q], 1)
                statistics(q, it, "t4", "bn4")

            def ln4(q, it):
                normalise(q, it, hid[q], "rs4")

            rounds(dve, "dve", {"adj_transpose": x_split, "adj_split": adj_split, "K": k_low, "Z": evacuate("Zh"), "U": hidden,
                         "h_transpose": hidden_low, "P": v_rows, "y": t1, "ln1": ln1, "Z1": evacuate("Z1h"),
                         "X1": evacuate_relu("X1h"), "S2": evacuate("S2h"), "X2": evacuate_relu("X2h"),
                         "S3": evacuate("S3h"), "o3": t2, "ln2": ln2, "x2_transpose": evacuate("x2Th"), "S": s_low,
                         "agg": t3, "ln3": ln3, "x3_transpose": evacuate("x3Th"), "Y": y3_low, "scores": leaky,
                         "attn": a_low, "R": t4, "ln4": ln4})

        @block.gpsimd
        def _(pool):
            nc.gpsimd.memset(ident[:, :], 0.0).then_inc(const_set, 1)
            pool.wait_ge(const_set, 1)
            nc.gpsimd.affine_select(out=ident[:, :], in_=ident[:, :], compare_op=ALU.not_equal, fill=1.0, base=0,
                                    pattern=[[-1, P]], channel_multiplier=1)
            nc.gpsimd.memset(ones[:, :], 1.0)
            nc.gpsimd.memset(pick[:, 0:1], 1.0)
            nc.gpsimd.memset(pick[:, 1:2], -1.0)
            nc.gpsimd.memset(minus_half[:, :], -0.5)
            nc.gpsimd.memset(eps_col[:, :], EPS_LN)
            nc.gpsimd.memset(f32(ones_row[:, :]), 1.0)
            for q in range(LANES):
                nc.gpsimd.memset(f32(rows[q][0][:, :, F:F + 1]), 1.0)
                nc.gpsimd.memset(f32(rows[q][0][:, :, F + 1:F + 2]), 0.0)
                nc.gpsimd.memset(f32(rows[q][1][:, :, F:F + 2]), 0.0)
            nc.gpsimd.memset(f32(wp[0][:, :, F:F + 2]), 0.0)
            nc.gpsimd.memset(f32(wp[1][:, :, F:F + 2]), 0.0).then_inc(const_set, 1)
            pool.wait_ge(const_set, 2)
            nc.gpsimd.memset(pick[0:1, 0:1], 0.0)
            nc.gpsimd.memset(pick[0:1, 1:2], 1.0).then_inc(const_set, 1)
            pool.wait_ge(const_set, 3)

            def own(q, name, it):
                pool.wait_ge(gp_done[q], done(GP, name, it))

            def adj_low(q, it):
                pool.wait_ge(dv_done[q], done(DV, "aTh", it))
                nc.gpsimd.tensor_tensor(aT[q][1][:, :, :], a_buf[q][:, :, :], f32(aT[q][0][:, :, :]),
                                        ALU.subtract).then_inc(gp_done[q], 1)
                pool.wait_ge(dv_done[q], done(DV, "Beh", it))
                nc.gpsimd.tensor_tensor(BH[q][0], f32(HT[q]), f32(bc[q][0][:, :]).unsqueeze(2).to_broadcast([P, T, N]),
                                        ALU.mult).then_inc(gp_done[q], 1)

            def root(aggr, eps):
                def step(q, it):
                    pool.wait_ge(dv_done[q], done(DV, aggr, it))
                    nc.gpsimd.tensor_tensor(col(q, VE), mv(q)[:, :, 1], eps_col[:, :], ALU.add).then_inc(gp_done[q], 1)
                    own(q, eps, it)
                    nc.gpsimd.tensor_tensor(col(q, RS), col(q, VE), minus_half[:, :], ALU.pow).then_inc(gp_done[q], 1)
                return step

            def v_low(q, it):
                pool.wait_ge(sc_done[q], done(SC, "Vh", it))
                nc.gpsimd.tensor_tensor(op[q][1][:, :, :], hid[q][:, 0:T, :], f32(op[q][0][:, :, :]),
                                        ALU.subtract).then_inc(gp_done[q], 1)

            def x1_low(q, it):
                pool.wait_ge(dv_done[q], done(DV, "x1h", it))
                nc.gpsimd.tensor_tensor(rows[q][1][:, :, 0:F], cur[q][:, :, :], f32(rows[q][0][:, :, 0:F]),
                                        ALU.subtract).then_inc(gp_done[q], 1)
                nc.gpsimd.tensor_tensor(tmp[q][:, :, :], cur[q][:, :, :],
                                        c3_t[:, :].unsqueeze(1).to_broadcast([P, T, F]), ALU.add).then_inc(gp_done[q], 1)

            def attention(q, it):
                pool.wait_ge(sc_done[q], done(SC, "exp", it))
                nc.gpsimd.tensor_tensor(A_[q], E_[q], a_buf[q][:, :, :], ALU.mult).then_inc(gp_done[q], 1)

            rounds(pool, "pool", {"adj_split": adj_low, "U": root("aggrh", "epsh"), "P": v_low, "y": root("aggr1", "eps1"),
                          "ln1": x1_low, "o3": root("aggr2", "eps2"), "agg": root("aggr3", "eps3"),
                          "attn": attention, "R": root("aggr4", "eps4")})


def kernel(**inputs):
    import numpy as _np
    import concourse.bacc as _bacc
    from concourse import mybir as _mybir
    from concourse.bass_utils import run_bass_kernel_spmd as _run

    a = {k: _np.asarray(v) for k, v in inputs.items()}
    laid = {
        "x": a["x"], "adj": a["adj"],
        "W1T": a["L0_gnn_W1"].T, "b1": a["L0_gnn_b1"], "gamma": a["L0_gnn_gamma"].reshape(-1, 128).T,
        "beta": a["L0_gnn_beta"].reshape(-1, 128).T, "W2T": a["L0_gnn_W2"].T, "b2": a["L0_gnn_b2"],
        "C1": a["L1_gnn_W1"], "c1": a["L1_gnn_b1"], "C2": a["L1_gnn_W2"], "c2": a["L1_gnn_b2"],
        "C3": a["L1_gnn_W3"], "c3": a["L1_gnn_b3"], "WT": a["L2_gnn_W"].T, "w": a["L3_gnn_w"], "a": a["L3_gnn_a"],
    }
    nc = _bacc.Bacc("TRN2", target_bir_lowering=False, num_devices=1)
    arrays, args = {}, []
    for name, v in laid.items():
        v = _np.ascontiguousarray(v)
        arrays[f"in_{name}_dram"] = v
        args.append(nc.dram_tensor(f"in_{name}_dram", v.shape, _mybir.dt.from_np(v.dtype), kind="ExternalInput").ap())
    args.append(nc.dram_tensor("out_0_dram", a["x"].shape, _mybir.dt.from_np(_np.dtype("float32")),
                               kind="ExternalOutput").ap())
    graph_layers(nc, *args)
    r = _run(nc, [arrays], core_ids=[0])
    return r.results[0]["out_0_dram"]
```

```python
from contextlib import ExitStack

import concourse.bass as bass
from concourse import mybir

F32 = mybir.dt.float32
F32R = mybir.dt.float32r
ALU = mybir.AluOpType
ACT = mybir.ActivationFunctionType
AX = mybir.AxisListType

P = 128
LANES = 4
EPS_LN = 1e-5
EPS_DEG = 1e-6
TINY = 1e-38

ORDER_SP = """load_adj 0, load_x 0, store 4"""
ORDER_PE = """Z1 2, agg 3, U0 1, X1 2, U1 1, S2 2, adjT 0, hT 1, X2 2, x3T 3, P 1, S3 2, Y 3, o3 2,
    s_row 3, K 0, y 1, Z 0, x2T 2, R 3, S 2, P1 2"""
ORDER_SC = """Kh 1, exp 4, Ah 4, x2 3, Zh 1, x2Th 3, x1 2, Sh 3, P1c 3, Z1h 2, X1h 2, out 4, xh 0, h 1,
    S2h 2, aT 0, hTh 1, x3 3, aTh 0, X2h 2, x3Th 3, S3h 2, Yh 3, Vh 1, tanh 3"""
ORDER_DV = """eps1 2, x2Tl 3, nb1 2, xa 1, rrec 4, x1h 2, q 4, x1l 2, t4 4, Sl 3, Zl 1, bn4 4, aggr4 4,
    Z1l 2, deg 3, degc 3, eps4 4, rdeg 3, u 3, Upre0 1, nb4 4, t3 3, X1l 2, Upre1 1, bn3 3, xl 0,
    aggr3 3, eps3 3, S2l 2, HT 0, nb3 3, cmax 0, hTl 1, Be 0, bnh 1, aggrh 1, X2l 2, x1b 2,
    epsh 1, x3Tl 3, Beh 0, V 1, S3l 2, Bel 0, w_col 0, BHl 0, s8 3, Yl 3, t2 2, bn2 2, leaky 3,
    dmax 0, aggr2 2, Kl 0, drec 0, A 3, Dn 0, nb2 2, t1 1, bn1 1, aggr1 1"""
ORDER_GP = """Al 4, rs1 2, rs4 4, rs3 3, aTl 0, rsh 1, BHh 0, Vl 1, eps2 2, rs2 2"""


def table(order):
    return [(x.split()[0], int(x.split()[1])) for x in order.replace("\n", " ").split(",")]


def of_one_graph(order):
    return [step for step, age in sorted(table(order), key=lambda x: x[1])]


PE, SC, DV, GP = (of_one_graph(x) for x in (ORDER_PE, ORDER_SC, ORDER_DV, ORDER_GP))


class Round:

    def __init__(self, eng, index, behind=0, bases=None, scratch=None):
        self.eng, self.index, self.behind, self.bases, self.scratch = eng, index, behind, bases, scratch
        self.number = None if bases else index - behind
        self.first = self.number == 0
        self.graph = index - behind

    def last(self):
        return Round(self.eng, self.index, self.behind + 1, self.bases, self.scratch)

    def count(self, each, plus):
        if self.bases is None:
            return self.number * each + plus
        if plus == self.behind * each:
            return self.bases[each]
        self.eng.reg_add(self.scratch, self.bases[each], plus - self.behind * each)
        return self.scratch


def done(steps, name, it):
    return it.count(len(steps), steps.index(name) + 1)


def graph_layers(nc, x, adj, W1T, b1, gamma, beta, W2T, b2, C1, c1, C2, c2, C3, c3, WT, w, a, out):
    GRAPHS, N, F = x.shape
    FH = W1T.shape[1]
    T = N // P
    TH = FH // P
    ROUNDS = GRAPHS // LANES
    assert N == F == T * P and GRAPHS == ROUNDS * LANES

    with ExitStack() as ctx:
        def sb(name, shape, dt=F32):
            return ctx.enter_context(nc.sbuf_tensor(name, shape, dt))

        def sem(name):
            return ctx.enter_context(nc.semaphore(name))

        def per_lane(make):
            return [make(q) for q in range(LANES)]

        def pair(name, shape):
            return sb(name + "_high", shape, F32R), sb(name + "_low", shape, F32R)

        a_buf = per_lane(lambda q: sb(f"adj{q}", [P, T, N]))
        cur = per_lane(lambda q: sb(f"cur{q}", [P, T, F]))
        tmp = per_lane(lambda q: sb(f"tmp{q}", [P, T, F]))
        aT = per_lane(lambda q: pair(f"aT{q}", [P, T, N]))
        K = per_lane(lambda q: pair(f"K{q}", [P, T, N]))
        op = per_lane(lambda q: pair(f"op{q}", [P, T, N]))
        rows = per_lane(lambda q: pair(f"rows{q}", [P, T, F + 2]))
        hid = per_lane(lambda q: sb(f"hid{q}", [P, 2 * T, F]))
        big = per_lane(lambda q: pair(f"big{q}", [P, TH, N]))
        small = per_lane(lambda q: sb(f"small{q}", [P, 64]))
        bc = per_lane(lambda q: pair(f"inv_count{q}", [P, T]))
        ps = per_lane(lambda q: ctx.enter_context(nc.psum_tensor(f"ps{q}", [P, 2, 512], F32)))

        W1p = pair("W1T", [P, T, FH])
        W2p = pair("W2T", [P, TH, F])
        Cp = [pair(f"C{n}", [P, T, F]) for n in (1, 2, 3)]
        WTp = pair("WT", [P, 2 * T, F])
        wp = pair("w3", [P, T, F + 2])
        b1_t = sb("b1_t", [P, FH])
        bb_t = sb("bb_t", [P, F])
        b2_t = sb("b2_t", [P, F])
        c3_t = sb("c3_t", [P, F])
        ident = sb("ident", [P, P])
        ones = sb("ones", [P, P])
        ones_row = sb("ones_row", [2, N], F32R)
        c_raw = sb("c_raw", [2, 2 * F])
        c_high = sb("c_high", [2, 2 * F], F32R)
        c_mid = sb("c_mid", [2, 2 * F])
        c_row = sb("c_row", [2, 2 * F], F32R)
        pick = sb("pick", [2, 2])
        minus_half = sb("minus_half", [P, T])
        eps_col = sb("eps_col", [P, T])
        gam = sb("gam", [P, TH])
        bet = sb("bet", [P, TH])
        vcol = sb("vcol", [P, T])

        pe_done = per_lane(lambda q: sem(f"pe_done{q}"))
        sc_done = per_lane(lambda q: sem(f"sc_done{q}"))
        dv_done = per_lane(lambda q: sem(f"dv_done{q}"))
        gp_done = per_lane(lambda q: sem(f"gp_done{q}"))
        adj_in = per_lane(lambda q: sem(f"adj_in{q}"))
        x_in = per_lane(lambda q: sem(f"x_in{q}"))
        stored = per_lane(lambda q: sem(f"stored{q}"))
        w_in = sem("w_in")
        const_set = sem("const_set")
        w_high = sem("w_high")
        w_dve = sem("w_dve")
        w_pe = sem("w_pe")
        w_centred = sem("w_centred")

        def after(step, q, it):
            for steps, sems in ((PE, pe_done), (SC, sc_done), (DV, dv_done), (GP, gp_done)):
                if step in steps:
                    return sems[q], done(steps, step, it)

        def st(q):
            return small[q][:, 0:12].rearrange("p (t s) -> p t s", t=T)

        def mv(q):
            return small[q][:, 12:16].rearrange("p (t s) -> p t s", t=T)

        def col(q, n):
            return small[q][:, 16 + 2 * n:18 + 2 * n]
        VE, RS, CNT, CMAX, BE, DMAX, DREC, DN, DEG, DEGC, RDEG, RREC, QQ, S8, NB = range(15)

        def f32(t):
            return t.bitcast(F32)

        HT = [op[q][0][:, :, :] for q in range(LANES)]
        BH = [tuple(v[:, :, :].rearrange("p t n -> p (t n)")[:, 0:T * (N + 2)].rearrange("p (t n) -> p t n", t=T)
                    for v in big[q]) for q in range(LANES)]
        AP_ = [(big[q][0][:, 0:T, :], big[q][1][:, 0:T, :]) for q in range(LANES)]
        E_ = [hid[q][:, 0:T, :] for q in range(LANES)]
        A_ = [hid[q][:, T:2 * T, :] for q in range(LANES)]
        h512 = [hid[q][:, :, :].rearrange("p (t u) f -> p t (u f)", t=T) for q in range(LANES)]
        bank = [[ps[q][:, b, :].rearrange("p (t f) -> p t f", t=T) for b in range(2)] for q in range(LANES)]

        raw = {"W1": h512[0], "W2": hid[1][:, :, :], "WT": hid[2][:, :, :], "C0": tmp[0][:, :, :],
               "C1": tmp[1][:, :, :], "C2": tmp[2][:, :, :], "w": tmp[3][:, :, :], "a": hid[3][:, 0, :],
               "prod": hid[3][:, 1, :]}

        def windows(eng, name, order, step_of):
            steps = table(order)
            oldest = max(age for _, age in steps)
            kinds = sorted({len(PE), len(SC), len(DV), len(GP), 16})

            def window(i, w, bases, scratch):
                for step, age in steps:
                    q, behind = (w - age) % LANES, int(w < age)
                    if bases is None and not 0 <= (i - behind) * LANES + q < GRAPHS:
                        continue
                    step_of[step](q, Round(eng, i, behind, bases, scratch))

            for w in range(LANES):
                window(0, w, None, None)
            scratch = eng.alloc_register(f"{name}_value")
            bases = {each: eng.alloc_register(f"{name}_rounds_x{each}") for each in kinds}
            for each in kinds:
                eng.reg_mov(bases[each], each)
            with eng.Fori(1, ROUNDS) as i:
                for w in range(LANES):
                    window(i, w, bases, scratch)
                for each in kinds:
                    eng.reg_add(bases[each], bases[each], each)
            for w in range(oldest):
                window(ROUNDS, w, None, None)

        W_DONE = 13
        def copies(eng, copy, signal):
            def rows_high(source):
                def step(q, it):
                    if source:
                        eng.wait_ge(*after(source, q, it))
                    else:
                        eng.wait_ge(x_in[q], it.count(16, 16))
                    copy(rows[q][0][:, :, 0:F], cur[q][:, :, :]).then_inc(signal[q], 1)
                return step

            def v_high(q, it):
                eng.wait_ge(*after("V", q, it))
                copy(op[q][0][:, :, :], hid[q][:, 0:T, :]).then_inc(signal[q], 1)

            def p1_copy(q, it):
                eng.wait_ge(*after("P1", q, it))
                copy(hid[q][:, 0:T, :], bank[q][1]).then_inc(signal[q], 1)

            def a_high(q, it):
                eng.wait_ge(*after("A", q, it))
                copy(AP_[q][0], A_[q]).then_inc(signal[q], 1)

            return {"xh": rows_high(None), "x1h": rows_high("x1"), "Vh": v_high, "P1c": p1_copy, "Ah": a_high}

        def elementwise(eng, unit, signal):
            def rows_low(high):
                def step(q, it):
                    eng.wait_ge(*after(high, q, it))
                    unit.tensor_tensor(rows[q][1][:, :, 0:F], cur[q][:, :, :], f32(rows[q][0][:, :, 0:F]),
                                       ALU.subtract).then_inc(signal[q], 1)
                return step

            def adj_low(q, it):
                eng.wait_ge(*after("aT", q, it))
                eng.wait_ge(*after("aTh", q, it))
                unit.tensor_tensor(aT[q][1][:, :, :], a_buf[q][:, :, :], f32(aT[q][0][:, :, :]),
                                   ALU.subtract).then_inc(signal[q], 1)

            def scaled(part, needs):
                def step(q, it):
                    eng.wait_ge(*after(needs, q, it))
                    unit.tensor_tensor(BH[q][part][:, :, 0:N], f32(HT[q]),
                                       f32(bc[q][part][:, :]).unsqueeze(2).to_broadcast([P, T, N]),
                                       ALU.mult).then_inc(signal[q], 1)
                return step

            def add_eps(aggr):
                def step(q, it):
                    eng.wait_ge(*after(aggr, q, it))
                    unit.tensor_tensor(col(q, VE), mv(q)[:, :, 1], eps_col[:, :], ALU.add).then_inc(signal[q], 1)
                return step

            def v_low(q, it):
                eng.wait_ge(*after("Vh", q, it))
                unit.tensor_tensor(op[q][1][:, :, :], hid[q][:, 0:T, :], f32(op[q][0][:, :, :]),
                                   ALU.subtract).then_inc(signal[q], 1)

            def x1_and_bias(q, it):
                eng.wait_ge(*after("x1", q, it))
                unit.tensor_tensor(tmp[q][:, :, :], cur[q][:, :, :], c3_t[:, :].unsqueeze(1).to_broadcast([P, T, F]),
                                   ALU.add).then_inc(signal[q], 1)

            def attention(q, it):
                eng.wait_ge(*after("exp", q, it))
                unit.tensor_tensor(A_[q], E_[q], a_buf[q][:, :, :], ALU.mult).then_inc(signal[q], 1)

            def attention_low(q, it):
                eng.wait_ge(*after("Ah", q, it))
                unit.tensor_tensor(AP_[q][1], A_[q], f32(AP_[q][0]), ALU.subtract).then_inc(signal[q], 1)

            return {"xl": rows_low("xh"), "x1l": rows_low("x1h"), "aTl": adj_low, "BHh": scaled(0, "Beh"),
                    "BHl": scaled(1, "Bel"), "epsh": add_eps("aggrh"), "eps1": add_eps("aggr1"),
                    "eps2": add_eps("aggr2"), "eps3": add_eps("aggr3"), "eps4": add_eps("aggr4"), "Vl": v_low,
                    "x1b": x1_and_bias, "A": attention, "Al": attention_low}

        block = ctx.enter_context(nc.Block())

        @block.sync
        def _(sp):
            def tiles(w_, t):
                return w_.rearrange("(t p) f -> p t f", t=t)

            def over_rows(v, n):
                return v.rearrange("(a n) -> a n", a=1).to_broadcast([P, n])
            for dst, src in ((raw["W1"], tiles(W1T, T)), (raw["W2"], tiles(W2T, TH)), (raw["WT"], tiles(WT, 2 * T)),
                             (raw["C0"], tiles(C1, T)), (raw["C1"], tiles(C2, T)), (raw["C2"], tiles(C3, T)),
                             (raw["w"], tiles(w, T)),
                             (raw["a"], over_rows(a, F)), (b1_t[:, :], over_rows(b1, FH)),
                             (b2_t[:, :], over_rows(b2, F)), (c3_t[:, :], over_rows(c3, F)),
                             (gam[:, :], gamma), (bet[:, :], beta)):
                sp.dma_start(dst, src).then_inc(w_in, 16)
            for n, c in enumerate((c1, c2)):
                for r in range(2):
                    sp.dma_start(c_raw[r:r + 1, n * F:(n + 1) * F],
                                 c.rearrange("(a n) -> a n", a=1)).then_inc(w_in, 16)

            def rows_of(t, q, it):
                return t[bass.ds(it.graph * LANES + q, 1), :, :].rearrange("g (t p) n -> p (g t) n", p=P)

            def load_adj(q, it):
                if it.first:
                    sp.wait_ge(w_dve, W_DONE)
                else:
                    sp.wait_ge(*after("A", q, it.last()))
                sp.dma_start(a_buf[q][:, :, :], rows_of(adj, q, it)).then_inc(adj_in[q], 16)

            def load_x(q, it):
                if not it.first:
                    sp.wait_ge(*after("t4", q, it.last()))
                sp.dma_start(cur[q][:, :, :], rows_of(x, q, it)).then_inc(x_in[q], 16)

            def store(q, it):
                sp.wait_ge(*after("out", q, it))
                sp.dma_start(rows_of(out, q, it), hid[q][:, 0:T, :]).then_inc(stored[q], 16)

            windows(sp, "sp", ORDER_SP, {"load_adj": load_adj, "load_x": load_x, "store": store})
            for q in range(LANES):
                sp.wait_ge(stored[q], 16 * ROUNDS)

        @block.tensor
        def _(pe):
            def product(dst, left, right, contract, cols, bias=None, passes=((1, 0), (0, 1), (0, 0))):
                for m, d in enumerate(dst):
                    if bias is not None:
                        nc.tensor.matmul(d, c_row[:, bias + m * P:bias + (m + 1) * P], ones_row[:, :],
                                         start=True, stop=False)
                    for n, (i, j) in enumerate(passes):
                        for k in range(contract):
                            last = nc.tensor.matmul(d, left[i][:, k, m * P:(m + 1) * P], right[j][:, k, 0:cols],
                                                    start=(bias is None and n == 0 and k == 0),
                                                    stop=(n == len(passes) - 1 and k == contract - 1))
                return last

            pe.wait_ge(const_set, 2)
            pe.wait_ge(w_dve, 2)
            for k in range(TH):
                nc.tensor.matmul(ps[0][:, 0, 0:F], ones[:, :], hid[0][:, k, :], start=(k == 0), stop=(k == TH - 1))
            for k in range(TH):
                last = nc.tensor.matmul(ps[0][:, 1, 0:F], bet[:, k:k + 1].to_broadcast([P, P]), raw["W2"][:, k, :],
                                        start=(k == 0), stop=(k == TH - 1))
            last.then_inc(w_pe, 1)
            pe.wait_ge(w_dve, W_DONE)
            pe.wait_ge(w_high, 6)

            def banks(q):
                return [ps[q][:, b, 0:F + 2] for b in range(2)]

            def tiles(q, b=0):
                return [bank[q][b][:, t, :] for t in range(T)]

            def adj_transpose(q, it):
                pe.wait_ge(adj_in[q], it.count(16, 16))
                if not it.first:
                    pe.wait_ge(*after("t4", q, it.last()))
                for t in range(T):
                    for u in range(T):
                        last = nc.tensor.transpose(bank[q][0][:, t, u * P:(u + 1) * P],
                                                   a_buf[q][:, u, t * P:(t + 1) * P], ident[:, :])
                last.then_inc(pe_done[q], 1)

            def k_product(q, it):
                pe.wait_ge(*after("BHh", q, it))
                pe.wait_ge(*after("BHl", q, it))
                pe.wait_ge(*after("w_col", q, it))
                pe.wait_ge(*after("aT", q, it))
                pe.wait_ge(*after("aTh", q, it))
                product(banks(q), (HT[q],), BH[q], T, N + 2, passes=[(0, 1), (0, 0)]).then_inc(pe_done[q], 1)

            def z_product(q, it):
                pe.wait_ge(*after("Kh", q, it))
                pe.wait_ge(*after("Kl", q, it))
                pe.wait_ge(*after("Dn", q, it))
                pe.wait_ge(*after("xl", q, it))
                product(tiles(q), rows[q], K[q], T, N).then_inc(pe_done[q], 1)

            def u_product(m):
                def step(q, it):
                    pe.wait_ge(*after("Zh", q, it))
                    pe.wait_ge(*after("Zl", q, it))
                    left = [v[:, :, m * P:(m + 1) * P] for v in op[q]]
                    product([ps[q][:, m, :]], left, W1p, T, FH).then_inc(pe_done[q], 1)
                return step

            def h_transpose(q, it):
                pe.wait_ge(*after("h", q, it))
                for f in range(TH):
                    for t in range(T):
                        last = nc.tensor.transpose(bank[q][f // 2][:, f % 2, t * P:(t + 1) * P],
                                                   h512[q][:, t, f * P:(f + 1) * P], ident[:, :])
                last.then_inc(pe_done[q], 1)

            def p_product(q, it):
                pe.wait_ge(*after("hTh", q, it))
                pe.wait_ge(*after("hTl", q, it))
                product(tiles(q), big[q], W2p, TH, F).then_inc(pe_done[q], 1)

            def y_product(q, it):
                pe.wait_ge(*after("Vh", q, it))
                pe.wait_ge(*after("Vl", q, it))
                product(tiles(q), K[q], op[q], T, F).then_inc(pe_done[q], 1)

            def z1_product(q, it):
                pe.wait_ge(*after("x1h", q, it))
                pe.wait_ge(*after("x1l", q, it))
                pe.wait_ge(*after("aTl", q, it))
                product(tiles(q), rows[q], aT[q], T, N).then_inc(pe_done[q], 1)

            def x1_product(q, it):
                pe.wait_ge(*after("Z1h", q, it))
                pe.wait_ge(*after("Z1l", q, it))
                product(tiles(q), Cp[0], op[q], T, N, bias=0).then_inc(pe_done[q], 1)

            def s2_product(q, it):
                pe.wait_ge(*after("X1h", q, it))
                pe.wait_ge(*after("X1l", q, it))
                product(tiles(q), op[q], Cp[1], T, F).then_inc(pe_done[q], 1)

            def x2_product(q, it):
                pe.wait_ge(*after("S2h", q, it))
                pe.wait_ge(*after("S2l", q, it))
                product(tiles(q), op[q], aT[q], T, N, bias=F).then_inc(pe_done[q], 1)

            def s3_product(q, it):
                pe.wait_ge(*after("X2h", q, it))
                pe.wait_ge(*after("X2l", q, it))
                product(tiles(q), op[q], Cp[2], T, F).then_inc(pe_done[q], 1)

            def o3_product(q, it):
                pe.wait_ge(*after("S3h", q, it))
                pe.wait_ge(*after("S3l", q, it))
                product(tiles(q), aT[q], op[q], T, F).then_inc(pe_done[q], 1)

            def cur_transpose(q):
                for f in range(T):
                    for t in range(T):
                        last = nc.tensor.transpose(bank[q][0][:, f, t * P:(t + 1) * P],
                                                   cur[q][:, t, f * P:(f + 1) * P], ident[:, :])
                last.then_inc(pe_done[q], 1)

            def x2_transpose(q, it):
                pe.wait_ge(*after("x2", q, it))
                cur_transpose(q)

            def s_product(q, it):
                pe.wait_ge(*after("x2Th", q, it))
                pe.wait_ge(*after("x2Tl", q, it))
                product(tiles(q), op[q], [v[:, T:2 * T, :] for v in WTp], T, F).then_inc(pe_done[q], 1)

            def p1_product(q, it):
                pe.wait_ge(*after("x2Th", q, it))
                pe.wait_ge(*after("x2Tl", q, it))
                product(tiles(q, 1), op[q], [v[:, 0:T, :] for v in WTp], T, F).then_inc(pe_done[q], 1)

            def agg_product(q, it):
                pe.wait_ge(*after("Sh", q, it))
                pe.wait_ge(*after("P1c", q, it))
                pe.wait_ge(*after("Sl", q, it))
                product(banks(q), aT[q], rows[q], T, F + 2).then_inc(pe_done[q], 1)

            def x3_transpose(q, it):
                pe.wait_ge(*after("x3", q, it))
                cur_transpose(q)

            def y3_product(q, it):
                pe.wait_ge(*after("x3Th", q, it))
                pe.wait_ge(*after("x3Tl", q, it))
                product(banks(q), op[q], wp, T, F + 2).then_inc(pe_done[q], 1)

            def s_row(q, it):
                pe.wait_ge(*after("s8", q, it))
                pe.wait_ge(*after("Yl", q, it))
                for t in range(T):
                    last = nc.tensor.transpose(bank[q][0][:, 0, t * P:(t + 1) * P],
                                               col(q, S8)[:, t:t + 1].to_broadcast([P, P]), ident[:, :])
                last.then_inc(pe_done[q], 1)

            def r_product(q, it):
                pe.wait_ge(*after("Ah", q, it))
                pe.wait_ge(*after("Al", q, it))
                pe.wait_ge(*after("Yl", q, it))
                product(banks(q), AP_[q], rows[q], T, F + 2).then_inc(pe_done[q], 1)

            windows(pe, "pe", ORDER_PE, {
                "adjT": adj_transpose, "K": k_product, "Z": z_product, "U0": u_product(0), "U1": u_product(1),
                "hT": h_transpose, "P": p_product, "y": y_product, "Z1": z1_product, "X1": x1_product,
                "S2": s2_product, "X2": x2_product, "S3": s3_product, "o3": o3_product, "x2T": x2_transpose,
                "S": s_product, "P1": p1_product, "agg": agg_product, "x3T": x3_transpose, "Y": y3_product,
                "s_row": s_row, "R": r_product})

        @block.scalar
        def _(act):
            act.wait_ge(w_in, 16 * 17)
            for v, src in ((W1p, raw["W1"]), (WTp, raw["WT"]), (Cp[0], raw["C0"]), (Cp[1], raw["C1"]),
                           (Cp[2], raw["C2"])):
                nc.scalar.activation(v[0][:, :, :], src, ACT.Copy).then_inc(w_high, 1)
            nc.scalar.activation(wp[0][:, :, 0:F], raw["w"], ACT.Copy).then_inc(w_high, 1)

            def adj_copy(q, it):
                act.wait_ge(*after("adjT", q, it))
                nc.scalar.activation(a_buf[q][:, :, :], bank[q][0], ACT.Copy).then_inc(sc_done[q], 1)

            def adj_high(q, it):
                act.wait_ge(*after("adjT", q, it))
                nc.scalar.activation(aT[q][0][:, :, :], bank[q][0], ACT.Copy).then_inc(sc_done[q], 1)

            def normalise(n, into):
                def step(q, it):
                    act.wait_ge(*after(f"nb{n}", q, it))
                    for t in range(T):
                        last = nc.scalar.activation(into[q][:, t, :], tmp[q][:, t, :], ACT.Identity,
                                                    bias=col(q, NB)[:, t:t + 1], scale=col(q, RS)[:, t:t + 1])
                    last.then_inc(sc_done[q], 1)
                return step

            def k_high(q, it):
                act.wait_ge(*after("K", q, it))
                nc.scalar.activation(K[q][0][:, :, :], ps[q][:, :, 0:N], ACT.Copy).then_inc(sc_done[q], 1)

            def evacuate(name, func=ACT.Copy):
                def step(q, it):
                    act.wait_ge(*after(name, q, it))
                    nc.scalar.activation(op[q][0][:, :, :], bank[q][0], func).then_inc(sc_done[q], 1)
                return step

            def hidden_relu(q, it):
                act.wait_ge(*after("Upre0", q, it))
                act.wait_ge(*after("Upre1", q, it))
                nc.scalar.activation(hid[q][:, :, :], hid[q][:, :, :], ACT.Relu).then_inc(sc_done[q], 1)

            def hidden_high(q, it):
                act.wait_ge(*after("hT", q, it))
                nc.scalar.activation(big[q][0][:, :, :], ps[q][:, :, :].rearrange("p b (t n) -> p (b t) n", t=T), ACT.Copy).then_inc(sc_done[q], 1)

            def s_high(q, it):
                act.wait_ge(*after("S", q, it))
                nc.scalar.activation(rows[q][0][:, :, 0:F], bank[q][0], ACT.Copy).then_inc(sc_done[q], 1)

            def y3_high(q, it):
                act.wait_ge(*after("Y", q, it))
                nc.scalar.activation(rows[q][0][:, :, 0:F], ps[q][:, :, 0:F], ACT.Copy).then_inc(sc_done[q], 1)

            def scores(q, it):
                act.wait_ge(*after("s_row", q, it))
                for t in range(T):
                    last = nc.scalar.activation(tmp[q][:, t, :], ps[q][:, 0, 0:N], ACT.Tanh, bias=col(q, S8)[:, t:t + 1])
                last.then_inc(sc_done[q], 1)

            def exponential(q, it):
                act.wait_ge(*after("leaky", q, it))
                nc.scalar.activation(E_[q], tmp[q][:, :, :], ACT.Exp, scale=8.0).then_inc(sc_done[q], 1)

            windows(act, "act", ORDER_SC, {
                **copies(act, lambda o, i: nc.scalar.activation(o, i, ACT.Copy), sc_done),
                "aT": adj_copy, "aTh": adj_high, "Kh": k_high, "Zh": evacuate("Z"), "h": hidden_relu,
                "hTh": hidden_high, "x1": normalise(1, cur), "Z1h": evacuate("Z1"),
                "X1h": evacuate("X1", ACT.Relu), "S2h": evacuate("S2"), "X2h": evacuate("X2", ACT.Relu),
                "S3h": evacuate("S3"), "x2": normalise(2, cur), "x2Th": evacuate("x2T"), "Sh": s_high,
                "x3": normalise(3, cur), "x3Th": evacuate("x3T"), "Yh": y3_high, "tanh": scores,
                "exp": exponential, "out": normalise(4, hid)})

        @block.vector
        def _(dve):
            dve.wait_ge(w_in, 16 * 17)
            dve.wait_ge(w_high, 1)
            nc.vector.tensor_tensor(W1p[1][:, :, :], raw["W1"], f32(W1p[0][:, :, :]), ALU.subtract).then_inc(w_dve, 1)
            dve.wait_ge(w_dve, 1)
            for k in range(TH):
                last = nc.vector.tensor_scalar(hid[0][:, k, :], raw["W2"][:, k, :], gam[:, k:k + 1], None, ALU.mult)
            last.then_inc(w_dve, 1)
            dve.wait_ge(w_high, 6)
            for v, src in ((WTp, raw["WT"]), (Cp[0], raw["C0"]), (Cp[1], raw["C1"]), (Cp[2], raw["C2"])):
                last = nc.vector.tensor_tensor(v[1][:, :, :], src, f32(v[0][:, :, :]), ALU.subtract)
            nc.vector.tensor_tensor(wp[1][:, :, 0:F], raw["w"], f32(wp[0][:, :, 0:F]), ALU.subtract).then_inc(w_dve, 1)
            for k in range(T):
                nc.vector.tensor_tensor(hid[3][:, 1 + k, :], raw["w"][:, k, :], raw["a"], ALU.mult).then_inc(w_dve, 1)
            dve.wait_ge(w_dve, 5)
            nc.vector.reduce_sum(vcol[:, :], hid[3][:, 1:1 + T, :], AX.X).then_inc(w_dve, 1)
            dve.wait_ge(w_dve, 6)
            dve.wait_ge(const_set, 3)
            nc.vector.tensor_copy(wp[0][:, :, F:F + 1], vcol[:, :].unsqueeze(2)).then_inc(w_dve, 1)
            dve.wait_ge(w_dve, 7)
            nc.vector.tensor_tensor(wp[1][:, :, F:F + 1], vcol[:, :].unsqueeze(2), f32(wp[0][:, :, F:F + 1]),
                                    ALU.subtract).then_inc(w_dve, 1)
            nc.vector.tensor_copy(c_high[:, :], c_raw[:, :]).then_inc(w_dve, 1)
            dve.wait_ge(w_dve, 9)
            nc.vector.tensor_scalar(c_mid[:, :], f32(c_high[:, :]), pick[:, 1:2], None, ALU.mult).then_inc(w_dve, 1)
            dve.wait_ge(w_dve, 10)
            nc.vector.scalar_tensor_tensor(c_row[:, :], c_raw[:, :], pick[:, 0:1], c_mid[:, :], ALU.mult,
                                           ALU.add).then_inc(w_dve, 1)
            dve.wait_ge(w_pe, 1)
            nc.vector.tensor_copy(bb_t[:, :], ps[0][:, 1, 0:F])
            for k in range(TH):
                last = nc.vector.scalar_tensor_tensor(hid[1][:, k, :], ps[0][:, 0, 0:F], -1.0 / FH, hid[0][:, k, :],
                                                      ALU.mult, ALU.add)
            last.then_inc(w_dve, 1)
            dve.wait_ge(w_dve, 12)
            nc.vector.tensor_copy(W2p[0][:, :, :], hid[1][:, :, :]).then_inc(w_centred, 1)
            dve.wait_ge(w_centred, 1)
            nc.vector.tensor_tensor(W2p[1][:, :, :], hid[1][:, :, :], f32(W2p[0][:, :, :]),
                                    ALU.subtract).then_inc(w_dve, 1)
            dve.wait_ge(w_dve, W_DONE)

            def own(q, name, it):
                dve.wait_ge(*after(name, q, it))

            def twice_x(q, it):
                dve.wait_ge(*after("xh", q, it))
                dve.wait_ge(*after("xl", q, it))
                for t in range(T):
                    last = nc.vector.scalar_tensor_tensor(cur[q][:, t, :], cur[q][:, t, :], 2.0, b2_t[:, :],
                                                          ALU.mult, ALU.add)
                last.then_inc(dv_done[q], 1)

            def incidence(q, it):
                dve.wait_ge(*after("aT", q, it))
                for k in range(T):
                    last = nc.vector.tensor_scalar(HT[q][:, k, :], a_buf[q][:, k, :], 0.0, 0.0, ALU.not_equal,
                                                   ALU.add, accum_out=col(q, CNT)[:, k:k + 1])
                last.then_inc(dv_done[q], 1)

            def count_max(q, it):
                own(q, "HT", it)
                nc.vector.tensor_scalar(col(q, CMAX), col(q, CNT), 1.0, None, ALU.max).then_inc(dv_done[q], 1)

            def count_inverse(q, it):
                own(q, "cmax", it)
                nc.vector.reciprocal(col(q, BE), col(q, CMAX)).then_inc(dv_done[q], 1)

            def count_high(q, it):
                own(q, "Be", it)
                nc.vector.tensor_copy(bc[q][0][:, :], col(q, BE)).then_inc(dv_done[q], 1)

            def count_low(q, it):
                own(q, "Beh", it)
                nc.vector.tensor_tensor(bc[q][1][:, :], col(q, BE), f32(bc[q][0][:, :]), ALU.subtract)\
                    .then_inc(dv_done[q], 1)

            def w_column(q, it):
                dve.wait_ge(*after("aTh", q, it))
                nc.vector.tensor_copy(BH[q][0][:, :, N:N + 2], f32(aT[q][0][:, :, 0:2]))
                dve.wait_ge(*after("aTl", q, it))
                nc.vector.tensor_copy(BH[q][1][:, :, N:N + 2], f32(aT[q][1][:, :, 0:2])).then_inc(dv_done[q], 1)

            def d_max(q, it):
                dve.wait_ge(*after("Kh", q, it))
                nc.vector.tensor_scalar(col(q, DMAX), ps[q][:, :, N], TINY, None, ALU.max).then_inc(dv_done[q], 1)

            def d_inverse(q, it):
                own(q, "dmax", it)
                nc.vector.reciprocal(col(q, DREC), col(q, DMAX)).then_inc(dv_done[q], 1)

            def d_where(q, it):
                own(q, "drec", it)
                nc.vector.scalar_tensor_tensor(col(q, DN), ps[q][:, :, N], 0.0, col(q, DREC), ALU.is_gt, ALU.mult)\
                    .then_inc(dv_done[q], 1)

            def k_low(q, it):
                dve.wait_ge(*after("Kh", q, it))
                nc.vector.tensor_tensor(K[q][1][:, :, :], ps[q][:, :, 0:N], f32(K[q][0][:, :, :]), ALU.subtract)\
                    .then_inc(dv_done[q], 1)

            def evacuate(high):
                def step(q, it):
                    dve.wait_ge(*after(high, q, it))
                    nc.vector.tensor_tensor(op[q][1][:, :, :], bank[q][0], f32(op[q][0][:, :, :]),
                                            ALU.subtract).then_inc(dv_done[q], 1)
                return step

            def evacuate_relu(high):
                def step(q, it):
                    dve.wait_ge(*after(high, q, it))
                    nc.vector.scalar_tensor_tensor(op[q][1][:, :, :], bank[q][0], 0.0, f32(op[q][0][:, :, :]),
                                                   ALU.max, ALU.subtract).then_inc(dv_done[q], 1)
                return step

            def hidden(t):
                def step(q, it):
                    if not it.first:
                        dve.wait_ge(stored[q], it.count(16, 0))
                    own(q, "Dn", it)
                    dve.wait_ge(*after(f"U{t}", q, it))
                    nc.vector.scalar_tensor_tensor(h512[q][:, t, :], ps[q][:, t, :], col(q, DN)[:, t:t + 1],
                                                   b1_t[:, :], ALU.mult, ALU.add).then_inc(dv_done[q], 1)
                return step

            def hidden_statistics(q, it):
                dve.wait_ge(*after("h", q, it))
                for t in range(T):
                    last = nc.vector.bn_stats(st(q)[:, t, :], h512[q][:, t, :])
                last.then_inc(dv_done[q], 1)

            def statistics(before):
                def step(q, it):
                    own(q, before, it)
                    for t in range(T):
                        last = nc.vector.bn_stats(st(q)[:, t, :], tmp[q][:, t, :])
                    last.then_inc(dv_done[q], 1)
                return step

            def aggregate(stats):
                def step(q, it):
                    own(q, stats, it)
                    nc.vector.tensor_copy(small[q][:, 60:61], st(q)[:, 0, 0:1])
                    for t in range(T):
                        last = nc.vector.bn_aggr(mv(q)[:, t, :], st(q)[:, t, :])
                    last.then_inc(dv_done[q], 1)
                return step

            def shift(n):
                def step(q, it):
                    dve.wait_ge(*after(f"rs{n}", q, it))
                    nc.vector.scalar_tensor_tensor(col(q, NB), mv(q)[:, :, 0], -1.0, col(q, RS), ALU.mult, ALU.mult)\
                        .then_inc(dv_done[q], 1)
                return step

            def hidden_low(q, it):
                dve.wait_ge(*after("hTh", q, it))
                nc.vector.tensor_tensor(big[q][1][:, :, :], ps[q][:, :, :].rearrange("p b (t n) -> p (b t) n", t=T),
                                        f32(big[q][0][:, :, :]), ALU.subtract).then_inc(dv_done[q], 1)

            def v_rows(q, it):
                dve.wait_ge(*after("P", q, it))
                dve.wait_ge(*after("rsh", q, it))
                for t in range(T):
                    last = nc.vector.scalar_tensor_tensor(hid[q][:, t, :], bank[q][0][:, t, :], col(q, RS)[:, t:t + 1],
                                                          bb_t[:, :], ALU.mult, ALU.add)
                last.then_inc(dv_done[q], 1)

            def t1(q, it):
                own(q, "xa", it)
                dve.wait_ge(*after("y", q, it))
                for t in range(T):
                    last = nc.vector.scalar_tensor_tensor(tmp[q][:, t, :], bank[q][0][:, t, :], col(q, DN)[:, t:t + 1],
                                                          cur[q][:, t, :], ALU.mult, ALU.add)
                last.then_inc(dv_done[q], 1)

            def t2(q, it):
                dve.wait_ge(*after("o3", q, it))
                dve.wait_ge(*after("x1b", q, it))
                nc.vector.tensor_tensor(tmp[q][:, :, :], bank[q][0], tmp[q][:, :, :], ALU.add).then_inc(dv_done[q], 1)

            def s_low(q, it):
                dve.wait_ge(*after("Sh", q, it))
                nc.vector.tensor_tensor(rows[q][1][:, :, 0:F], bank[q][0], f32(rows[q][0][:, :, 0:F]),
                                        ALU.subtract).then_inc(dv_done[q], 1)

            def degree(q, it):
                dve.wait_ge(*after("agg", q, it))
                nc.vector.tensor_copy(col(q, DEG), ps[q][:, :, F]).then_inc(dv_done[q], 1)

            def degree_max(q, it):
                own(q, "deg", it)
                nc.vector.tensor_scalar(col(q, DEGC), col(q, DEG), EPS_DEG, None, ALU.max).then_inc(dv_done[q], 1)

            def degree_inverse(q, it):
                own(q, "degc", it)
                nc.vector.reciprocal(col(q, RDEG), col(q, DEGC)).then_inc(dv_done[q], 1)

            def mean_aggregate(q, it):
                own(q, "rdeg", it)
                for t in range(T):
                    last = nc.vector.scalar_tensor_tensor(hid[q][:, T + t, :], ps[q][:, t, 0:F],
                                                          col(q, RDEG)[:, t:t + 1], hid[q][:, t, :], ALU.mult, ALU.add)
                last.then_inc(dv_done[q], 1)

            def t3(q, it):
                own(q, "u", it)
                nc.vector.scalar_tensor_tensor(tmp[q][:, :, :], hid[q][:, T:2 * T, :], 0.0, cur[q][:, :, :],
                                               ALU.max, ALU.add).then_inc(dv_done[q], 1)

            def s8(q, it):
                dve.wait_ge(*after("Yh", q, it))
                nc.vector.tensor_scalar(col(q, S8), ps[q][:, :, F], 0.125, None, ALU.mult).then_inc(dv_done[q], 1)

            def y3_low(q, it):
                dve.wait_ge(*after("Yh", q, it))
                nc.vector.tensor_tensor(rows[q][1][:, :, 0:F], ps[q][:, :, 0:F], f32(rows[q][0][:, :, 0:F]),
                                        ALU.subtract).then_inc(dv_done[q], 1)

            def leaky(q, it):
                dve.wait_ge(*after("tanh", q, it))
                nc.vector.scalar_tensor_tensor(tmp[q][:, :, :], tmp[q][:, :, :], 0.1, tmp[q][:, :, :], ALU.mult,
                                               ALU.max).then_inc(dv_done[q], 1)

            def r_inverse(q, it):
                dve.wait_ge(*after("R", q, it))
                nc.vector.reciprocal(col(q, RREC), ps[q][:, :, F]).then_inc(dv_done[q], 1)

            def r_scale(q, it):
                own(q, "rrec", it)
                nc.vector.tensor_tensor(col(q, QQ), col(q, RREC), col(q, DEG), ALU.mult).then_inc(dv_done[q], 1)

            def t4(q, it):
                own(q, "q", it)
                for t in range(T):
                    last = nc.vector.scalar_tensor_tensor(tmp[q][:, t, :], ps[q][:, t, 0:F], col(q, QQ)[:, t:t + 1],
                                                          cur[q][:, t, :], ALU.mult, ALU.add)
                last.then_inc(dv_done[q], 1)

            windows(dve, "dve", ORDER_DV, {
                **copies(dve, nc.vector.tensor_copy, dv_done), **elementwise(dve, nc.vector, dv_done),
                "xa": twice_x, "HT": incidence, "cmax": count_max, "Be": count_inverse, "Beh": count_high,
                "Bel": count_low, "w_col": w_column, "dmax": d_max, "drec": d_inverse, "Dn": d_where,
                "Kl": k_low, "Zl": evacuate("Zh"), "Upre0": hidden(0), "Upre1": hidden(1),
                "bnh": hidden_statistics, "aggrh": aggregate("bnh"), "hTl": hidden_low, "V": v_rows,
                "t1": t1, "bn1": statistics("t1"), "aggr1": aggregate("bn1"), "nb1": shift(1),
                "Z1l": evacuate("Z1h"), "X1l": evacuate_relu("X1h"), "S2l": evacuate("S2h"),
                "X2l": evacuate_relu("X2h"), "S3l": evacuate("S3h"), "t2": t2, "bn2": statistics("t2"),
                "aggr2": aggregate("bn2"), "nb2": shift(2), "x2Tl": evacuate("x2Th"), "Sl": s_low,
                "deg": degree, "degc": degree_max, "rdeg": degree_inverse, "u": mean_aggregate, "t3": t3,
                "bn3": statistics("t3"), "aggr3": aggregate("bn3"), "nb3": shift(3), "x3Tl": evacuate("x3Th"),
                "s8": s8, "Yl": y3_low, "leaky": leaky, "rrec": r_inverse, "q": r_scale, "t4": t4,
                "bn4": statistics("t4"), "aggr4": aggregate("bn4"), "nb4": shift(4)})

        @block.gpsimd
        def _(pool):
            nc.gpsimd.memset(ident[:, :], 0.0).then_inc(const_set, 1)
            pool.wait_ge(const_set, 1)
            nc.gpsimd.affine_select(out=ident[:, :], in_=ident[:, :], compare_op=ALU.not_equal, fill=1.0, base=0,
                                    pattern=[[-1, P]], channel_multiplier=1)
            nc.gpsimd.memset(ones[:, :], 1.0)
            nc.gpsimd.memset(pick[:, 0:1], 1.0)
            nc.gpsimd.memset(pick[:, 1:2], -1.0)
            nc.gpsimd.memset(minus_half[:, :], -0.5)
            nc.gpsimd.memset(eps_col[:, :], EPS_LN)
            nc.gpsimd.memset(f32(ones_row[:, :]), 1.0)
            for q in range(LANES):
                nc.gpsimd.memset(f32(rows[q][0][:, :, F:F + 1]), 1.0)
                nc.gpsimd.memset(f32(rows[q][0][:, :, F + 1:F + 2]), 0.0)
                nc.gpsimd.memset(f32(rows[q][1][:, :, F:F + 2]), 0.0)
            nc.gpsimd.memset(f32(wp[0][:, :, F:F + 2]), 0.0)
            nc.gpsimd.memset(f32(wp[1][:, :, F:F + 2]), 0.0).then_inc(const_set, 1)
            pool.wait_ge(const_set, 2)
            nc.gpsimd.memset(pick[0:1, 0:1], 0.0)
            nc.gpsimd.memset(pick[0:1, 1:2], 1.0).then_inc(const_set, 1)
            pool.wait_ge(const_set, 3)

            def own(q, name, it):
                pool.wait_ge(*after(name, q, it))

            def root(eps):
                def step(q, it):
                    own(q, eps, it)
                    nc.gpsimd.tensor_tensor(col(q, RS), col(q, VE), minus_half[:, :], ALU.pow).then_inc(gp_done[q], 1)
                return step

            windows(pool, "pool", ORDER_GP, {
                **elementwise(pool, nc.gpsimd, gp_done), "rsh": root("epsh"), "rs1": root("eps1"),
                "rs2": root("eps2"), "rs3": root("eps3"), "rs4": root("eps4")})


def kernel(**inputs):
    import numpy as _np
    import concourse.bacc as _bacc
    from concourse import mybir as _mybir
    from concourse.bass_utils import run_bass_kernel_spmd as _run

    a = {k: _np.asarray(v) for k, v in inputs.items()}
    laid = {
        "x": a["x"], "adj": a["adj"],
        "W1T": a["L0_gnn_W1"].T, "b1": a["L0_gnn_b1"], "gamma": a["L0_gnn_gamma"].reshape(-1, 128).T,
        "beta": a["L0_gnn_beta"].reshape(-1, 128).T, "W2T": a["L0_gnn_W2"].T, "b2": a["L0_gnn_b2"],
        "C1": a["L1_gnn_W1"], "c1": a["L1_gnn_b1"], "C2": a["L1_gnn_W2"], "c2": a["L1_gnn_b2"],
        "C3": a["L1_gnn_W3"], "c3": a["L1_gnn_b3"], "WT": a["L2_gnn_W"].T, "w": a["L3_gnn_w"], "a": a["L3_gnn_a"],
    }
    nc = _bacc.Bacc("TRN2", target_bir_lowering=False, num_devices=1)
    arrays, args = {}, []
    for name, v in laid.items():
        v = _np.ascontiguousarray(v)
        arrays[f"in_{name}_dram"] = v
        args.append(nc.dram_tensor(f"in_{name}_dram", v.shape, _mybir.dt.from_np(v.dtype), kind="ExternalInput").ap())
    args.append(nc.dram_tensor("out_0_dram", a["x"].shape, _mybir.dt.from_np(_np.dtype("float32")),
                               kind="ExternalOutput").ap())
    graph_layers(nc, *args)
    r = _run(nc, [arrays], core_ids=[0])
    return r.results[0]["out_0_dram"]
```

```python
from contextlib import ExitStack

import concourse.bass as bass
from concourse import mybir

F32 = mybir.dt.float32
F32R = mybir.dt.float32r
ALU = mybir.AluOpType
ACT = mybir.ActivationFunctionType
AX = mybir.AxisListType

P = 128
LANES = 4
PEELED = 2
EPS_LN = 1e-5
EPS_DEG = 1e-6
TINY = 1e-30
LEAST = 1.2e-38

ORDER_SP = """load_adj 0, load_x 0, store 4"""
ORDER_PE = """U0 1, Z1a 2, Z1 2, hT1 1, hT0 1, X1a 2, x2T 3, Ra 4, R 4, X1 2, Sa 3, S 3, P1 3, S2a 2, S2 2,
    agga 3, agg 3, Pa 1, X2a 2, X2 2, Pm 1, Pb 1, Ka 0, K 0, S3a 2, x3T 3, ya 1, y 1, S3 2, Ya 3,
    Y 3, Z 0, o3a 2, o3 2, U1a 0, U1 0, s_row 3"""
ORDER_SC = """S2h 2, out 4, X2f 2, xh 0, X2h 2, Vh 1, Kh 0, x3Th 3, S3h 2, Yh 3, Zh 0, x1h 1, tanh 3,
    exp 3, Z1h 1, h 0, x2Th 2, hTh0 0, X1f 1, X1h 1, Sh 2, hTh1 0, P1c 2"""
ORDER_DV = """hTl0 1, bn4 4, aggrh 1, aggr4 4, Sl 3, hTl1 1, nb4 4, aTh 0, HT 0, S2l 2, degc 3, Be 0,
    rdeg 3, u 3, Beh 0, t3 3, Bel 0, bn3 3, w_col 0, aggr3 3, eps3 3, V 1, x3 3, Vl 1, dmax 0,
    Kl 0, drec 0, x3Tl 3, t1 1, Dn 0, bn1 1, aggr1 1, S3l 2, Yl 3, x1 1, Zl 0, s8 3, t2 2, bn2 2,
    Upre1 0, aggr2 2, leaky 3, Upre0 0, x2 2, A 3, Z1l 1, Al 3, bnh 0, x2Tl 2, rrec 3, q 3, t4 3"""
ORDER_GP = """xb 1, eps1 2, rs1 2, x1l 2, eps2 3, rs2 3, Ah 4, x1b 2, X1l 2, epsh 1, eps4 4, rs4 4, rsh 1,
    aTl 0, BHh 0, BHl 0, rs3 3, xa 1, X2l 2, xl 0"""


def table(order):
    return [(x.split()[0], int(x.split()[1])) for x in order.replace("\n", " ").split(",")]


def of_one_graph(order):
    return [step for step, age in sorted(table(order), key=lambda x: x[1])]


PE, SC, DV, GP = (of_one_graph(x) for x in (ORDER_PE, ORDER_SC, ORDER_DV, ORDER_GP))


class Round:

    def __init__(self, eng, index, behind=0, bases=None, scratch=None):
        self.eng, self.index, self.behind, self.bases, self.scratch = eng, index, behind, bases, scratch
        self.number = None if bases else index - behind
        self.first = self.number == 0
        self.graph = index - behind

    def last(self):
        return Round(self.eng, self.index, self.behind + 1, self.bases, self.scratch)

    def count(self, each, plus):
        if self.bases is None:
            return self.number * each + plus
        if plus == self.behind * each:
            return self.bases[each]
        self.eng.reg_add(self.scratch, self.bases[each], plus - self.behind * each)
        return self.scratch


def done(steps, name, it):
    return it.count(len(steps), steps.index(name) + 1)


def graph_layers(nc, x, adjT, W1T, b1, gamma, beta, W2T, b2, C1, c1, C2, c2, C3, c3, WT, w, a, out):
    GRAPHS, N, F = x.shape
    FH = W1T.shape[1]
    T = N // P
    TH = FH // P
    ROUNDS = GRAPHS // LANES
    assert N == F == T * P and GRAPHS == ROUNDS * LANES

    with ExitStack() as ctx:
        def sb(name, shape, dt=F32):
            return ctx.enter_context(nc.sbuf_tensor(name, shape, dt))

        def sem(name):
            return ctx.enter_context(nc.semaphore(name))

        def per_lane(make):
            return [make(q) for q in range(LANES)]

        def pair(name, shape):
            return sb(name + "_high", shape, F32R), sb(name + "_low", shape, F32R)

        a_buf = per_lane(lambda q: sb(f"adj{q}", [P, T, N]))
        aT = per_lane(lambda q: pair(f"aT{q}", [P, T, N]))
        cur = per_lane(lambda q: sb(f"cur{q}", [P, T, F]))
        tmp = per_lane(lambda q: sb(f"tmp{q}", [P, T, F]))
        K = per_lane(lambda q: pair(f"K{q}", [P, T, N]))
        op = per_lane(lambda q: pair(f"op{q}", [P, T, N]))
        rows = per_lane(lambda q: pair(f"rows{q}", [P, T, F + 2]))
        hid = per_lane(lambda q: sb(f"hid{q}", [P, 2 * T, F]))
        big = per_lane(lambda q: pair(f"big{q}", [P, TH, N]))
        small = per_lane(lambda q: sb(f"small{q}", [P, 64]))
        bc = per_lane(lambda q: pair(f"inv_count{q}", [P, T]))
        ps = per_lane(lambda q: ctx.enter_context(nc.psum_tensor(f"ps{q}", [P, 2, 512], F32)))

        W1p = pair("W1T", [P, T, FH])
        W2p = pair("W2T", [P, TH, F])
        Cp = [pair(f"C{n}", [P, T, F]) for n in (1, 2, 3)]
        WTp = pair("WT", [P, 2 * T, F])
        wp = pair("w3", [P, T, F + 2])
        b1_t = sb("b1_t", [P, FH])
        bb_t = sb("bb_t", [P, F])
        b2_t = sb("b2_t", [P, F])
        c3_t = sb("c3_t", [P, F])
        ident = sb("ident", [P, P])
        ones = sb("ones", [P, P])
        minus_half = sb("minus_half", [P, T])
        eps_col = sb("eps_col", [P, T])
        c1_t = sb("c1_t", [P, T])
        c2_t = sb("c2_t", [P, T])
        gam = sb("gam", [P, TH])
        bet = sb("bet", [P, TH])
        vcol = sb("vcol", [P, T])
        a_t = sb("a_t", [P, F])

        pe_done = per_lane(lambda q: sem(f"pe_done{q}"))
        sc_done = per_lane(lambda q: sem(f"sc_done{q}"))
        dv_done = per_lane(lambda q: sem(f"dv_done{q}"))
        gp_done = per_lane(lambda q: sem(f"gp_done{q}"))
        adj_in = per_lane(lambda q: sem(f"adj_in{q}"))
        x_in = per_lane(lambda q: sem(f"x_in{q}"))
        stored = per_lane(lambda q: sem(f"stored{q}"))
        const_set = sem("const_set")
        tiles_in = sem("tiles_in")
        w1_in = sem("w1_in")
        w2_in = sem("w2_in")
        c_in = sem("c_in")
        wt_in = sem("wt_in")
        w_high = sem("w_high")
        w_dve = sem("w_dve")
        w_pe = sem("w_pe")

        def after(step, q, it):
            for steps, sems in ((PE, pe_done), (SC, sc_done), (DV, dv_done), (GP, gp_done)):
                if step in steps:
                    return sems[q], done(steps, step, it)

        def st(q):
            return small[q][:, 0:12].rearrange("p (t s) -> p t s", t=T)

        def mv(q):
            return small[q][:, 12:16].rearrange("p (t s) -> p t s", t=T)

        def col(q, n):
            return small[q][:, 16 + 2 * n:18 + 2 * n]
        VE, RS, CNT, BE, DMAX, DREC, DN, DEG, DEGC, RDEG, RREC, QQ, S8, NB = range(14)

        def f32(t):
            return t.bitcast(F32)

        HT = [op[q][0][:, :, :] for q in range(LANES)]
        BH = [tuple(v[:, :, :].rearrange("p t n -> p (t n)")[:, 0:T * (N + 2)].rearrange("p (t n) -> p t n", t=T)
                    for v in big[q]) for q in range(LANES)]
        AP_ = [(big[q][0][:, 0:T, :], big[q][1][:, 0:T, :]) for q in range(LANES)]
        E_ = [hid[q][:, 0:T, :] for q in range(LANES)]
        A_ = [hid[q][:, T:2 * T, :] for q in range(LANES)]
        h512 = [hid[q][:, :, :].rearrange("p (t u) f -> p t (u f)", t=T) for q in range(LANES)]
        bank = [[ps[q][:, b, :].rearrange("p (t f) -> p t f", t=T) for b in range(2)] for q in range(LANES)]

        raw_W1 = h512[1]
        raw_W2 = hid[2]
        gW2 = hid[3]
        raw_WT = (a_buf[2], a_buf[3])
        raw_C = (cur[2], cur[3], tmp[2])
        raw_w = tmp[3]
        GAMMA, W1_LOW, CENTRED, W2_HIGH, W2_LOW, C_LOW, W_LOW, VA, V_SUM, V_HIGH, W_DONE = range(1, 12)

        def windows(eng, name, order, step_of, before={}):
            steps = table(order)
            oldest = max(age for _, age in steps)
            kinds = sorted({len(PE), len(SC), len(DV), len(GP), 16})

            def window(i, w, bases, scratch):
                for step, age in steps:
                    q, behind = (w - age) % LANES, int(w < age)
                    if bases is None and not 0 <= (i - behind) * LANES + q < GRAPHS:
                        continue
                    it = Round(eng, i, behind, bases, scratch)
                    if q == 0 and it.first and step in before:
                        before[step]()
                    step_of[step](q, it)

            for i in range(PEELED):
                for w in range(LANES):
                    window(i, w, None, None)
            scratch = eng.alloc_register(f"{name}_value")
            bases = {each: eng.alloc_register(f"{name}_rounds_x{each}") for each in kinds}
            for each in kinds:
                eng.reg_mov(bases[each], PEELED * each)
            with eng.Fori(PEELED, ROUNDS) as i:
                for w in range(LANES):
                    window(i, w, bases, scratch)
                for each in kinds:
                    eng.reg_add(bases[each], bases[each], each)
            for w in range(oldest):
                window(ROUNDS, w, None, None)

        def copies(eng, copy, signal):
            def rows_high(source):
                def step(q, it):
                    if source:
                        eng.wait_ge(*after(source, q, it))
                    else:
                        eng.wait_ge(x_in[q], it.count(16, 16))
                    copy(rows[q][0][:, :, 0:F], cur[q][:, :, :]).then_inc(signal[q], 1)
                return step

            def adj_high(q, it):
                eng.wait_ge(adj_in[q], it.count(16, 16))
                copy(aT[q][0][:, :, :], a_buf[q][:, :, :]).then_inc(signal[q], 1)

            def hid_high(source):
                def step(q, it):
                    eng.wait_ge(*after(source, q, it))
                    copy(op[q][0][:, :, :], hid[q][:, 0:T, :]).then_inc(signal[q], 1)
                return step

            def p1_copy(q, it):
                eng.wait_ge(*after("P1", q, it))
                copy(hid[q][:, 0:T, :], bank[q][0]).then_inc(signal[q], 1)

            return {"aTh": adj_high, "xh": rows_high(None), "x1h": rows_high("x1"), "Vh": hid_high("V"),
                    "X1h": hid_high("X1f"), "X2h": hid_high("X2f"), "P1c": p1_copy}

        def elementwise(eng, unit, signal):
            def rows_low(high):
                def step(q, it):
                    eng.wait_ge(*after(high, q, it))
                    unit.tensor_tensor(rows[q][1][:, :, 0:F], cur[q][:, :, :], f32(rows[q][0][:, :, 0:F]),
                                       ALU.subtract).then_inc(signal[q], 1)
                return step

            def adj_low(q, it):
                eng.wait_ge(*after("aTh", q, it))
                unit.tensor_tensor(aT[q][1][:, :, :], a_buf[q][:, :, :], f32(aT[q][0][:, :, :]),
                                   ALU.subtract).then_inc(signal[q], 1)

            def scaled(part, needs):
                def step(q, it):
                    eng.wait_ge(*after(needs, q, it))
                    unit.tensor_tensor(BH[q][part][:, :, 0:N], f32(HT[q]),
                                       f32(bc[q][part][:, :]).unsqueeze(2).to_broadcast([P, T, N]),
                                       ALU.mult).then_inc(signal[q], 1)
                return step

            def add_eps(aggr):
                def step(q, it):
                    eng.wait_ge(*after(aggr, q, it))
                    unit.tensor_tensor(col(q, VE), mv(q)[:, :, 1], eps_col[:, :], ALU.add).then_inc(signal[q], 1)
                return step

            def hid_low(high):
                def step(q, it):
                    eng.wait_ge(*after(high, q, it))
                    unit.tensor_tensor(op[q][1][:, :, :], hid[q][:, 0:T, :], f32(op[q][0][:, :, :]),
                                       ALU.subtract).then_inc(signal[q], 1)
                return step

            def x1_and_bias(q, it):
                eng.wait_ge(*after("x1", q, it))
                unit.tensor_tensor(tmp[q][:, :, :], cur[q][:, :, :], c3_t[:, :].unsqueeze(1).to_broadcast([P, T, F]),
                                   ALU.add).then_inc(signal[q], 1)

            def x_and_bias(q, it):
                if it.first and q == 0:
                    eng.wait_ge(tiles_in, 16 * 3)
                eng.wait_ge(x_in[q], it.count(16, 16))
                if not it.first:
                    eng.wait_ge(*after("out", q, it.last()))
                elif q >= 2:
                    eng.wait_ge(w_dve, W_DONE)
                unit.tensor_tensor(tmp[q][:, :, :], cur[q][:, :, :], b2_t[:, :].unsqueeze(1).to_broadcast([P, T, F]),
                                   ALU.add).then_inc(signal[q], 1)

            def twice_x_and_bias(q, it):
                eng.wait_ge(*after("xb", q, it))
                unit.tensor_tensor(tmp[q][:, :, :], tmp[q][:, :, :], cur[q][:, :, :], ALU.add).then_inc(signal[q], 1)

            def attention(q, it):
                eng.wait_ge(*after("exp", q, it))
                unit.tensor_tensor(A_[q], E_[q], a_buf[q][:, :, :], ALU.mult).then_inc(signal[q], 1)

            def attention_high(q, it):
                eng.wait_ge(*after("exp", q, it))
                unit.tensor_tensor(AP_[q][0], E_[q], a_buf[q][:, :, :], ALU.mult).then_inc(signal[q], 1)

            def attention_low(q, it):
                eng.wait_ge(*after("A", q, it))
                eng.wait_ge(*after("Ah", q, it))
                unit.tensor_tensor(AP_[q][1], A_[q], f32(AP_[q][0]), ALU.subtract).then_inc(signal[q], 1)

            return {"xl": rows_low("xh"), "x1l": rows_low("x1h"), "aTl": adj_low, "BHh": scaled(0, "Beh"),
                    "BHl": scaled(1, "Bel"), "epsh": add_eps("aggrh"), "eps1": add_eps("aggr1"),
                    "eps2": add_eps("aggr2"), "eps3": add_eps("aggr3"), "eps4": add_eps("aggr4"), "Vl": hid_low("Vh"),
                    "X1l": hid_low("X1h"), "X2l": hid_low("X2h"),
                    "xb": x_and_bias,
                    "xa": twice_x_and_bias, "x1b": x1_and_bias, "A": attention, "Ah": attention_high,
                    "Al": attention_low}

        block = ctx.enter_context(nc.Block())

        @block.sync
        def _(sp):
            def tiles(w_, t):
                return w_.rearrange("(t p) f -> p t f", t=t)

            def over_rows(v, n):
                return v.rearrange("(a n) -> a n", a=1).to_broadcast([P, n])

            def rows_of(t, q, it):
                return t[bass.ds(it.graph * LANES + q, 1), :, :].rearrange("g (t p) n -> p (g t) n", p=P)

            def load_adj(q, it):
                if it.first:
                    if q >= 2:
                        sp.wait_ge(w_dve, W_DONE)
                else:
                    sp.wait_ge(*after("Al", q, it.last()))
                sp.dma_start(a_buf[q][:, :, :], rows_of(adjT, q, it)).then_inc(adj_in[q], 16)

            def load_x(q, it):
                if it.first:
                    if q >= 2:
                        sp.wait_ge(w_dve, W_DONE)
                else:
                    sp.wait_ge(*after("t4", q, it.last()))
                sp.dma_start(cur[q][:, :, :], rows_of(x, q, it)).then_inc(x_in[q], 16)

            def load_weights():
                sp.dma_start(b2_t[:, :], over_rows(b2, F)).then_inc(tiles_in, 16)
                sp.dma_start(raw_W2[:, :, :], tiles(W2T, TH)).then_inc(w2_in, 16)
                sp.dma_start(gam[:, :], gamma).then_inc(w2_in, 16)
                sp.dma_start(bet[:, :], beta).then_inc(w2_in, 16)
                sp.dma_start(raw_W1, tiles(W1T, T)).then_inc(w1_in, 16)
                sp.dma_start(b1_t[:, :], over_rows(b1, FH)).then_inc(tiles_in, 16)
                sp.dma_start(c3_t[:, :], over_rows(c3, F)).then_inc(tiles_in, 16)
                for raw, c in zip(raw_C, (C1, C2, C3)):
                    sp.dma_start(raw[:, :, :], tiles(c, T)).then_inc(c_in, 16)
                sp.dma_start(c1_t[:, :], c1).then_inc(c_in, 16)
                sp.dma_start(c2_t[:, :], c2).then_inc(c_in, 16)
                for n, raw in enumerate(raw_WT):
                    sp.dma_start(raw[:, :, :], tiles(WT[n * F:(n + 1) * F, :], T)).then_inc(wt_in, 16)
                sp.dma_start(raw_w[:, :, :], tiles(w, T)).then_inc(wt_in, 16)
                sp.dma_start(a_t[:, :], over_rows(a, F)).then_inc(wt_in, 16)

            def store(q, it):
                sp.wait_ge(*after("out", q, it))
                sp.dma_start(rows_of(out, q, it), hid[q][:, 0:T, :]).then_inc(stored[q], 16)

            def load_first(q, it):
                load_adj(q, it)
                if it.first and q == 0:
                    load_x(q, it)
                    load_weights()

            def load_x_later(q, it):
                if not (it.first and q == 0):
                    load_x(q, it)

            windows(sp, "sp", ORDER_SP, {"load_adj": load_first, "load_x": load_x_later, "store": store})
            for q in range(LANES):
                sp.wait_ge(stored[q], 16 * ROUNDS)

        @block.tensor
        def _(pe):
            def product(dst, left, right, contract, cols, passes=((0, 0), (0, 1), (1, 0)),
                        start=True, stop=True):
                ks = range(contract) if isinstance(contract, int) else contract
                for m, d, opens, closes in dst:
                    opens, closes = opens and start, closes and stop
                    for i, j in passes:
                        for k in ks:
                            last = nc.tensor.matmul(
                                d, left[i][:, k, m * P:(m + 1) * P], right[j][:, k, 0:cols],
                                start=opens and (i, j) == passes[0] and k == ks[0],
                                stop=closes and (i, j) == passes[-1] and k == ks[-1])
                return last

            LEFT_HIGH, LEFT_LOW = ((0, 0), (0, 1)), ((1, 0),)
            RIGHT_HIGH, RIGHT_LOW = ((0, 0), (1, 0)), ((0, 1),)

            def in_two(dst_of, left, right, cols, first_waits, high, low, low_ready, name):
                def start(q, it):
                    for step in first_waits:
                        pe.wait_ge(*after(step, q, it))
                    product(dst_of(q), left(q), right(q), T, cols, passes=high, stop=False).then_inc(pe_done[q], 1)

                def end(q, it):
                    pe.wait_ge(*after(low_ready, q, it))
                    product(dst_of(q), left(q), right(q), T, cols, passes=low, start=False).then_inc(pe_done[q], 1)
                return {name + "a": start, name: end}

            def w2_sums():
                pe.wait_ge(const_set, 2)
                pe.wait_ge(w_dve, GAMMA)
                for k in range(TH):
                    nc.tensor.matmul(ps[3][:, 0, 0:F], ones[:, :], gW2[:, k, :], start=(k == 0), stop=(k == TH - 1))
                for k in range(TH):
                    last = nc.tensor.matmul(ps[3][:, 1, 0:F], bet[:, k:k + 1].to_broadcast([P, P]), raw_W2[:, k, :],
                                            start=(k == 0), stop=(k == TH - 1))
                last.then_inc(w_pe, 1)
                pe.wait_ge(w_high, 1)
                pe.wait_ge(w_dve, W1_LOW)

            def w2_ready():
                pe.wait_ge(w_dve, W2_LOW)

            def c_ready():
                pe.wait_ge(w_high, 4)
                pe.wait_ge(w_dve, C_LOW)

            def wt_ready():
                pe.wait_ge(w_high, 7)
                pe.wait_ge(w_dve, W_DONE)

            def const_ready():
                pe.wait_ge(const_set, 2)

            def banks(q):
                return [(b, ps[q][:, b, 0:F + 2], True, True) for b in range(2)]

            def tiles(q, b=0):
                return [(t, bank[q][b][:, t, :], t == 0, t == T - 1) for t in range(T)]

            def tiles0(q):
                return tiles(q, 0)

            def tiles1(q):
                return tiles(q, 1)

            def k_start(q, it):
                pe.wait_ge(*after("BHh", q, it))
                pe.wait_ge(*after("w_col", q, it))
                product(banks(q), (HT[q],), BH[q], T, N + 2, passes=((0, 0),), stop=False).then_inc(pe_done[q], 1)

            def k_end(q, it):
                pe.wait_ge(*after("BHl", q, it))
                product(banks(q), (HT[q],), BH[q], T, N + 2, passes=((0, 1),), start=False).then_inc(pe_done[q], 1)

            def z_product(q, it):
                pe.wait_ge(*after("Kl", q, it))
                pe.wait_ge(*after("Dn", q, it))
                pe.wait_ge(*after("xl", q, it))
                product(tiles(q), rows[q], K[q], T, N).then_inc(pe_done[q], 1)

            def u_first(q, it):
                pe.wait_ge(*after("Zh", q, it))
                product([(1, ps[q][:, 1, :], True, True)], op[q], W1p, T, FH, passes=LEFT_HIGH,
                        stop=False).then_inc(pe_done[q], 1)

            def u_second(q, it):
                pe.wait_ge(*after("Zl", q, it))
                product([(1, ps[q][:, 1, :], True, True)], op[q], W1p, T, FH, passes=LEFT_LOW,
                        start=False).then_inc(pe_done[q], 1)

            def u_third(q, it):
                pe.wait_ge(*after("Zl", q, it))
                product([(0, ps[q][:, 0, :], True, True)], op[q], W1p, T, FH).then_inc(pe_done[q], 1)

            def h_transpose(b):
                def step(q, it):
                    pe.wait_ge(*after("Upre0", q, it))
                    pe.wait_ge(*after("Upre1", q, it))
                    for f in range(T * b, T * b + T):
                        for t in range(T):
                            last = nc.tensor.transpose(bank[q][b][:, f % T, t * P:(t + 1) * P],
                                                       h512[q][:, t, f * P:(f + 1) * P], ident[:, :])
                    last.then_inc(pe_done[q], 1)
                return step

            def p_start(q, it):
                pe.wait_ge(*after("hTl0", q, it))
                product(tiles(q), big[q], W2p, range(0, T), F, stop=False).then_inc(pe_done[q], 1)

            def p_middle(q, it):
                pe.wait_ge(*after("hTh1", q, it))
                product(tiles(q), big[q], W2p, range(T, TH), F, passes=LEFT_HIGH, start=False,
                        stop=False).then_inc(pe_done[q], 1)

            def p_end(q, it):
                pe.wait_ge(*after("hTl1", q, it))
                product(tiles(q), big[q], W2p, range(T, TH), F, passes=LEFT_LOW, start=False)\
                    .then_inc(pe_done[q], 1)

            def of(v):
                return lambda q: v

            chain = {
                **in_two(tiles0, K.__getitem__, op.__getitem__, F, ("Vh",), RIGHT_HIGH, RIGHT_LOW, "Vl", "y"),
                **in_two(tiles0, rows.__getitem__, aT.__getitem__, N, ("x1h", "aTl"), LEFT_HIGH, LEFT_LOW,
                         "x1l", "Z1"),
                **in_two(tiles1, of(Cp[0]), op.__getitem__, N, ("Z1h",), RIGHT_HIGH, RIGHT_LOW, "Z1l", "X1"),
                **in_two(tiles0, op.__getitem__, of(Cp[1]), F, ("X1h",), LEFT_HIGH, LEFT_LOW, "X1l", "S2"),
                **in_two(tiles1, op.__getitem__, aT.__getitem__, N, ("S2h",), LEFT_HIGH, LEFT_LOW, "S2l", "X2"),
                **in_two(tiles0, op.__getitem__, of(Cp[2]), F, ("X2h",), LEFT_HIGH, LEFT_LOW, "X2l", "S3"),
                **in_two(tiles1, aT.__getitem__, op.__getitem__, F, ("S3h",), RIGHT_HIGH, RIGHT_LOW, "S3l", "o3"),
                **in_two(tiles1, op.__getitem__, of([v[:, T:2 * T, :] for v in WTp]), F, ("x2Th",), LEFT_HIGH,
                         LEFT_LOW, "x2Tl", "S"),
                **in_two(banks, AP_.__getitem__, rows.__getitem__, F + 2, ("Ah",), LEFT_HIGH, LEFT_LOW, "Al", "R"),
            }

            def cur_transpose(q):
                for f in range(T):
                    for t in range(T):
                        last = nc.tensor.transpose(bank[q][0][:, f, t * P:(t + 1) * P],
                                                   cur[q][:, t, f * P:(f + 1) * P], ident[:, :])
                last.then_inc(pe_done[q], 1)

            def x2_transpose(q, it):
                pe.wait_ge(*after("x2", q, it))
                cur_transpose(q)

            def p1_product(q, it):
                pe.wait_ge(*after("x2Tl", q, it))
                product(tiles(q), op[q], [v[:, 0:T, :] for v in WTp], T, F).then_inc(pe_done[q], 1)

            def agg_start(q, it):
                pe.wait_ge(*after("Sl", q, it))
                product(banks(q)[1:], aT[q], rows[q], T, F + 2).then_inc(pe_done[q], 1)

            def agg_end(q, it):
                pe.wait_ge(*after("Sl", q, it))
                pe.wait_ge(*after("P1c", q, it))
                product(banks(q)[:1], aT[q], rows[q], T, F + 2).then_inc(pe_done[q], 1)

            def x3_transpose(q, it):
                pe.wait_ge(*after("x3", q, it))
                cur_transpose(q)

            def y3_start(q, it):
                pe.wait_ge(*after("x3Th", q, it))
                product(banks(q)[1:], op[q], wp, T, F + 2, passes=LEFT_HIGH, stop=False).then_inc(pe_done[q], 1)

            def y3_end(q, it):
                pe.wait_ge(*after("x3Tl", q, it))
                product(banks(q)[1:], op[q], wp, T, F + 2, passes=LEFT_LOW, start=False)
                product(banks(q)[:1], op[q], wp, T, F + 2).then_inc(pe_done[q], 1)

            def s_row(q, it):
                pe.wait_ge(*after("s8", q, it))
                pe.wait_ge(*after("Yl", q, it))
                for t in range(T):
                    last = nc.tensor.transpose(bank[q][0][:, 0, t * P:(t + 1) * P],
                                               col(q, S8)[:, t:t + 1].to_broadcast([P, P]), ident[:, :])
                last.then_inc(pe_done[q], 1)

            windows(pe, "pe", ORDER_PE, {
                "Ka": k_start, "K": k_end, "Z": z_product, "U1a": u_first, "U1": u_second,
                "U0": u_third, "hT0": h_transpose(0), "hT1": h_transpose(1), "Pa": p_start, "Pm": p_middle,
                "Pb": p_end, "x2T": x2_transpose, "P1": p1_product, "agga": agg_start, "agg": agg_end,
                "x3T": x3_transpose, "Ya": y3_start, "Y": y3_end, "s_row": s_row, **chain},
                before={"Ka": const_ready, "U1a": w2_sums, "Pa": w2_ready, "X1a": c_ready, "Sa": wt_ready,
                        "P1": wt_ready, "Ya": wt_ready})

        @block.scalar
        def _(act):
            def w1_high():
                act.wait_ge(w1_in, 16)
                nc.scalar.activation(W1p[0][:, :, :], raw_W1, ACT.Copy).then_inc(w_high, 1)

            def other_high():
                act.wait_ge(c_in, 16 * 5)
                for v, raw in zip(Cp, raw_C):
                    nc.scalar.activation(v[0][:, :, :], raw[:, :, :], ACT.Copy).then_inc(w_high, 1)
                act.wait_ge(wt_in, 16 * 4)
                for n, raw in enumerate(raw_WT):
                    nc.scalar.activation(WTp[0][:, T * n:T * n + T, :], raw[:, :, :], ACT.Copy).then_inc(w_high, 1)
                act.wait_ge(const_set, 2)
                nc.scalar.activation(wp[0][:, :, 0:F], raw_w[:, :, :], ACT.Copy).then_inc(w_high, 1)

            def output(q, it):
                act.wait_ge(*after("nb4", q, it))
                for t in range(T):
                    last = nc.scalar.activation(hid[q][:, t, :], tmp[q][:, t, :], ACT.Identity,
                                                bias=col(q, NB)[:, t:t + 1], scale=col(q, RS)[:, t:t + 1])
                last.then_inc(sc_done[q], 1)

            def k_high(q, it):
                act.wait_ge(*after("K", q, it))
                nc.scalar.activation(K[q][0][:, :, :], ps[q][:, :, 0:N], ACT.Copy).then_inc(sc_done[q], 1)

            def evacuate(name):
                def step(q, it):
                    act.wait_ge(*after(name, q, it))
                    nc.scalar.activation(op[q][0][:, :, :], bank[q][0], ACT.Copy).then_inc(sc_done[q], 1)
                return step

            def gcn(name, bias):
                def step(q, it):
                    act.wait_ge(*after(name, q, it))
                    for f in range(T):
                        last = nc.scalar.activation(hid[q][:, f, :], bank[q][1][:, f, :], ACT.Relu,
                                                    bias=bias[:, f:f + 1])
                    last.then_inc(sc_done[q], 1)
                return step

            def hidden_relu(q, it):
                act.wait_ge(*after("hT0", q, it))
                act.wait_ge(*after("hT1", q, it))
                nc.scalar.activation(hid[q][:, :, :], hid[q][:, :, :], ACT.Relu).then_inc(sc_done[q], 1)

            def hidden_high(b):
                def step(q, it):
                    act.wait_ge(*after(f"hT{b}", q, it))
                    nc.scalar.activation(big[q][0][:, T * b:T * b + T, :], bank[q][b],
                                         ACT.Relu).then_inc(sc_done[q], 1)
                return step

            def s_high(q, it):
                act.wait_ge(*after("S", q, it))
                nc.scalar.activation(rows[q][0][:, :, 0:F], bank[q][1], ACT.Copy).then_inc(sc_done[q], 1)

            def y3_high(q, it):
                act.wait_ge(*after("Y", q, it))
                nc.scalar.activation(rows[q][0][:, :, 0:F], ps[q][:, :, 0:F], ACT.Copy).then_inc(sc_done[q], 1)

            def scores(q, it):
                act.wait_ge(*after("s_row", q, it))
                for t in range(T):
                    last = nc.scalar.activation(tmp[q][:, t, :], ps[q][:, 0, 0:N], ACT.Tanh,
                                                bias=col(q, S8)[:, t:t + 1])
                last.then_inc(sc_done[q], 1)

            def exponential(q, it):
                act.wait_ge(*after("leaky", q, it))
                nc.scalar.activation(E_[q], tmp[q][:, :, :], ACT.Exp, scale=8.0).then_inc(sc_done[q], 1)

            windows(act, "act", ORDER_SC, {
                **copies(act, lambda o, i: nc.scalar.activation(o, i, ACT.Copy), sc_done),
                "Kh": k_high, "Zh": evacuate("Z"), "h": hidden_relu,
                "hTh0": hidden_high(0), "hTh1": hidden_high(1), "Z1h": evacuate("Z1"),
                "X1f": gcn("X1", c1_t), "S2h": evacuate("S2"), "X2f": gcn("X2", c2_t),
                "S3h": evacuate("S3"), "x2Th": evacuate("x2T"), "Sh": s_high,
                "x3Th": evacuate("x3T"), "Yh": y3_high, "tanh": scores,
                "exp": exponential, "out": output},
                before={"Zh": w1_high, "hTh0": other_high})

        @block.vector
        def _(dve):
            def gamma_w2():
                dve.wait_ge(w2_in, 16 * 3)
                for k in range(TH):
                    last = nc.vector.tensor_scalar(gW2[:, k, :], raw_W2[:, k, :], gam[:, k:k + 1], None, ALU.mult)
                last.then_inc(w_dve, 1)

            def w1_low():
                dve.wait_ge(w_high, 1)
                nc.vector.tensor_tensor(W1p[1][:, :, :], raw_W1, f32(W1p[0][:, :, :]), ALU.subtract)\
                    .then_inc(w_dve, 1)

            def centre_w2():
                dve.wait_ge(tiles_in, 16 * 3)
                dve.wait_ge(w_pe, 1)
                nc.vector.tensor_copy(bb_t[:, :], ps[3][:, 1, 0:F])
                for k in range(TH):
                    last = nc.vector.scalar_tensor_tensor(raw_W2[:, k, :], ps[3][:, 0, 0:F], -1.0 / FH, gW2[:, k, :],
                                                          ALU.mult, ALU.add)
                last.then_inc(w_dve, 1)
                dve.wait_ge(w_dve, CENTRED)
                nc.vector.tensor_copy(W2p[0][:, :, :], raw_W2[:, :, :]).then_inc(w_dve, 1)
                dve.wait_ge(w_dve, W2_HIGH)
                nc.vector.tensor_tensor(W2p[1][:, :, :], raw_W2[:, :, :], f32(W2p[0][:, :, :]),
                                        ALU.subtract).then_inc(w_dve, 1)

            def c_low():
                dve.wait_ge(w_high, 4)
                for v, raw in zip(Cp, raw_C):
                    last = nc.vector.tensor_tensor(v[1][:, :, :], raw[:, :, :], f32(v[0][:, :, :]), ALU.subtract)
                last.then_inc(w_dve, 1)

            def wt_low():
                dve.wait_ge(w_high, 7)
                for n, raw in enumerate(raw_WT):
                    nc.vector.tensor_tensor(WTp[1][:, T * n:T * n + T, :], raw[:, :, :],
                                            f32(WTp[0][:, T * n:T * n + T, :]), ALU.subtract)
                nc.vector.tensor_tensor(wp[1][:, :, 0:F], raw_w[:, :, :], f32(wp[0][:, :, 0:F]), ALU.subtract)\
                    .then_inc(w_dve, 1)
                dve.wait_ge(w_dve, W_LOW)
                nc.vector.tensor_tensor(raw_w[:, :, :], raw_w[:, :, :], a_t[:, :].unsqueeze(1).to_broadcast([P, T, F]),
                                        ALU.mult).then_inc(w_dve, 1)
                dve.wait_ge(w_dve, VA)
                nc.vector.reduce_sum(vcol[:, :], raw_w[:, :, :], AX.X).then_inc(w_dve, 1)
                dve.wait_ge(w_dve, V_SUM)
                nc.vector.tensor_copy(wp[0][:, :, F:F + 1], vcol[:, :].unsqueeze(2)).then_inc(w_dve, 1)
                dve.wait_ge(w_dve, V_HIGH)
                nc.vector.tensor_tensor(wp[1][:, :, F:F + 1], vcol[:, :].unsqueeze(2), f32(wp[0][:, :, F:F + 1]),
                                        ALU.subtract).then_inc(w_dve, 1)

            def const_ready():
                dve.wait_ge(const_set, 2)

            def own(q, name, it):
                dve.wait_ge(*after(name, q, it))

            def incidence(q, it):
                dve.wait_ge(adj_in[q], it.count(16, 16))
                if not it.first:
                    own(q, "t4", it.last())
                for k in range(T):
                    last = nc.vector.tensor_scalar(HT[q][:, k, :], a_buf[q][:, k, :], 0.0, TINY, ALU.not_equal,
                                                   ALU.add, accum_out=col(q, CNT)[:, k:k + 1])
                last.then_inc(dv_done[q], 1)

            def count_inverse(q, it):
                own(q, "HT", it)
                nc.vector.reciprocal(col(q, BE), col(q, CNT)).then_inc(dv_done[q], 1)

            def count_high(q, it):
                own(q, "Be", it)
                nc.vector.tensor_copy(bc[q][0][:, :], col(q, BE)).then_inc(dv_done[q], 1)

            def count_low(q, it):
                own(q, "Beh", it)
                nc.vector.tensor_tensor(bc[q][1][:, :], col(q, BE), f32(bc[q][0][:, :]), ALU.subtract)\
                    .then_inc(dv_done[q], 1)

            def w_column(q, it):
                own(q, "HT", it)
                dve.wait_ge(*after("aTh", q, it))
                nc.vector.tensor_copy(BH[q][0][:, :, N:N + 2], f32(aT[q][0][:, :, 0:2]))
                dve.wait_ge(*after("aTl", q, it))
                nc.vector.tensor_copy(BH[q][1][:, :, N:N + 2], f32(aT[q][1][:, :, 0:2])).then_inc(dv_done[q], 1)

            def d_max(q, it):
                dve.wait_ge(*after("Kh", q, it))
                nc.vector.tensor_scalar(col(q, DMAX), ps[q][:, :, N], LEAST, None, ALU.max).then_inc(dv_done[q], 1)

            def d_inverse(q, it):
                own(q, "dmax", it)
                nc.vector.reciprocal(col(q, DREC), col(q, DMAX)).then_inc(dv_done[q], 1)

            def d_where(q, it):
                own(q, "drec", it)
                nc.vector.scalar_tensor_tensor(col(q, DN), ps[q][:, :, N], 0.0, col(q, DREC), ALU.is_gt, ALU.mult)\
                    .then_inc(dv_done[q], 1)

            def k_low(q, it):
                dve.wait_ge(*after("Kh", q, it))
                nc.vector.tensor_tensor(K[q][1][:, :, :], ps[q][:, :, 0:N], f32(K[q][0][:, :, :]), ALU.subtract)\
                    .then_inc(dv_done[q], 1)

            def evacuate(high):
                def step(q, it):
                    dve.wait_ge(*after(high, q, it))
                    nc.vector.tensor_tensor(op[q][1][:, :, :], bank[q][0], f32(op[q][0][:, :, :]),
                                            ALU.subtract).then_inc(dv_done[q], 1)
                return step

            def hidden(t):
                def step(q, it):
                    if it.first:
                        dve.wait_ge(tiles_in, 16 * 3)
                    else:
                        dve.wait_ge(stored[q], it.count(16, 0))
                    dve.wait_ge(*after(f"U{t}", q, it))
                    nc.vector.scalar_tensor_tensor(h512[q][:, t, :], ps[q][:, t, :], col(q, DN)[:, t:t + 1],
                                                   b1_t[:, :], ALU.mult, ALU.add).then_inc(dv_done[q], 1)
                return step

            def hidden_statistics(q, it):
                dve.wait_ge(*after("h", q, it))
                for t in range(T):
                    last = nc.vector.bn_stats(st(q)[:, t, :], h512[q][:, t, :])
                last.then_inc(dv_done[q], 1)

            def statistics(before):
                def step(q, it):
                    own(q, before, it)
                    for t in range(T):
                        last = nc.vector.bn_stats(st(q)[:, t, :], tmp[q][:, t, :])
                    last.then_inc(dv_done[q], 1)
                return step

            def aggregate(stats):
                def step(q, it):
                    own(q, stats, it)
                    nc.vector.tensor_copy(small[q][:, 60:61], st(q)[:, 0, 0:1])
                    for t in range(T):
                        last = nc.vector.bn_aggr(mv(q)[:, t, :], st(q)[:, t, :])
                    last.then_inc(dv_done[q], 1)
                return step

            def normalise(n):
                def step(q, it):
                    dve.wait_ge(*after(f"rs{n}", q, it))
                    for t in range(T):
                        last = nc.vector.tensor_scalar(cur[q][:, t, :], tmp[q][:, t, :], mv(q)[:, t, 0:1],
                                                       col(q, RS)[:, t:t + 1], ALU.subtract, ALU.mult)
                    last.then_inc(dv_done[q], 1)
                return step

            def output_shift(q, it):
                dve.wait_ge(*after("rs4", q, it))
                nc.vector.scalar_tensor_tensor(col(q, NB), mv(q)[:, :, 0], -1.0, col(q, RS), ALU.mult, ALU.mult)\
                    .then_inc(dv_done[q], 1)

            def hidden_low(b):
                def step(q, it):
                    dve.wait_ge(*after(f"hTh{b}", q, it))
                    nc.vector.scalar_tensor_tensor(big[q][1][:, T * b:T * b + T, :], bank[q][b], 0.0,
                                                   f32(big[q][0][:, T * b:T * b + T, :]), ALU.max, ALU.subtract)\
                        .then_inc(dv_done[q], 1)
                return step

            def v_rows(q, it):
                dve.wait_ge(*after("Pb", q, it))
                dve.wait_ge(*after("rsh", q, it))
                for t in range(T):
                    last = nc.vector.scalar_tensor_tensor(hid[q][:, t, :], bank[q][0][:, t, :], col(q, RS)[:, t:t + 1],
                                                          bb_t[:, :], ALU.mult, ALU.add)
                last.then_inc(dv_done[q], 1)

            def t1(q, it):
                dve.wait_ge(*after("xa", q, it))
                dve.wait_ge(*after("y", q, it))
                for t in range(T):
                    last = nc.vector.scalar_tensor_tensor(tmp[q][:, t, :], bank[q][0][:, t, :], col(q, DN)[:, t:t + 1],
                                                          tmp[q][:, t, :], ALU.mult, ALU.add)
                last.then_inc(dv_done[q], 1)

            def t2(q, it):
                dve.wait_ge(*after("o3", q, it))
                dve.wait_ge(*after("x1b", q, it))
                nc.vector.tensor_tensor(tmp[q][:, :, :], bank[q][1], tmp[q][:, :, :], ALU.add).then_inc(dv_done[q], 1)

            def s_low(q, it):
                dve.wait_ge(*after("Sh", q, it))
                nc.vector.tensor_tensor(rows[q][1][:, :, 0:F], bank[q][1], f32(rows[q][0][:, :, 0:F]),
                                        ALU.subtract).then_inc(dv_done[q], 1)

            def degree_max(q, it):
                dve.wait_ge(*after("agg", q, it))
                nc.vector.tensor_copy(col(q, DEG), ps[q][:, :, F])
                nc.vector.tensor_scalar(col(q, DEGC), ps[q][:, :, F], EPS_DEG, None, ALU.max).then_inc(dv_done[q], 1)

            def degree_inverse(q, it):
                own(q, "degc", it)
                nc.vector.reciprocal(col(q, RDEG), col(q, DEGC)).then_inc(dv_done[q], 1)

            def mean_aggregate(q, it):
                own(q, "rdeg", it)
                for t in range(T):
                    last = nc.vector.scalar_tensor_tensor(hid[q][:, T + t, :], ps[q][:, t, 0:F],
                                                          col(q, RDEG)[:, t:t + 1], hid[q][:, t, :], ALU.mult, ALU.add)
                last.then_inc(dv_done[q], 1)

            def t3(q, it):
                own(q, "u", it)
                nc.vector.scalar_tensor_tensor(tmp[q][:, :, :], hid[q][:, T:2 * T, :], 0.0, cur[q][:, :, :],
                                               ALU.max, ALU.add).then_inc(dv_done[q], 1)

            def s8(q, it):
                dve.wait_ge(*after("Yh", q, it))
                nc.vector.tensor_scalar(col(q, S8), ps[q][:, :, F], 0.125, None, ALU.mult).then_inc(dv_done[q], 1)

            def y3_low(q, it):
                dve.wait_ge(*after("Yh", q, it))
                nc.vector.tensor_tensor(rows[q][1][:, :, 0:F], ps[q][:, :, 0:F], f32(rows[q][0][:, :, 0:F]),
                                        ALU.subtract).then_inc(dv_done[q], 1)

            def leaky(q, it):
                dve.wait_ge(*after("tanh", q, it))
                nc.vector.scalar_tensor_tensor(tmp[q][:, :, :], tmp[q][:, :, :], 0.1, tmp[q][:, :, :], ALU.mult,
                                               ALU.max).then_inc(dv_done[q], 1)

            def r_inverse(q, it):
                dve.wait_ge(*after("R", q, it))
                nc.vector.reciprocal(col(q, RREC), ps[q][:, :, F]).then_inc(dv_done[q], 1)

            def r_scale(q, it):
                own(q, "rrec", it)
                nc.vector.tensor_tensor(col(q, QQ), col(q, RREC), col(q, DEG), ALU.mult).then_inc(dv_done[q], 1)

            def t4(q, it):
                own(q, "q", it)
                for t in range(T):
                    last = nc.vector.scalar_tensor_tensor(tmp[q][:, t, :], ps[q][:, t, 0:F], col(q, QQ)[:, t:t + 1],
                                                          cur[q][:, t, :], ALU.mult, ALU.add)
                last.then_inc(dv_done[q], 1)

            windows(dve, "dve", ORDER_DV, {
                **copies(dve, nc.vector.tensor_copy, dv_done), **elementwise(dve, nc.vector, dv_done),
                "HT": incidence, "Be": count_inverse, "Beh": count_high,
                "Bel": count_low, "w_col": w_column, "dmax": d_max, "drec": d_inverse, "Dn": d_where,
                "Kl": k_low, "Zl": evacuate("Zh"), "Upre0": hidden(0), "Upre1": hidden(1),
                "bnh": hidden_statistics, "aggrh": aggregate("bnh"), "hTl0": hidden_low(0), "hTl1": hidden_low(1),
                "V": v_rows,
                "t1": t1, "bn1": statistics("t1"), "aggr1": aggregate("bn1"), "x1": normalise(1),
                "Z1l": evacuate("Z1h"), "S2l": evacuate("S2h"),
                "S3l": evacuate("S3h"), "t2": t2, "bn2": statistics("t2"),
                "aggr2": aggregate("bn2"), "x2": normalise(2), "x2Tl": evacuate("x2Th"), "Sl": s_low,
                "degc": degree_max, "rdeg": degree_inverse, "u": mean_aggregate, "t3": t3,
                "bn3": statistics("t3"), "aggr3": aggregate("bn3"), "x3": normalise(3), "x3Tl": evacuate("x3Th"),
                "s8": s8, "Yl": y3_low, "leaky": leaky, "rrec": r_inverse, "q": r_scale, "t4": t4,
                "bn4": statistics("t4"), "aggr4": aggregate("bn4"), "nb4": output_shift},
                before={"HT": const_ready, "dmax": gamma_w2, "Zl": w1_low, "Upre0": centre_w2, "V": c_low,
                        "t1": wt_low})

        @block.gpsimd
        def _(pool):
            nc.gpsimd.memset(ident[:, :], 0.0).then_inc(const_set, 1)
            pool.wait_ge(const_set, 1)
            nc.gpsimd.affine_select(out=ident[:, :], in_=ident[:, :], compare_op=ALU.not_equal, fill=1.0, base=0,
                                    pattern=[[-1, P]], channel_multiplier=1)
            nc.gpsimd.memset(ones[:, :], 1.0)
            nc.gpsimd.memset(minus_half[:, :], -0.5)
            nc.gpsimd.memset(eps_col[:, :], EPS_LN)
            for q in range(LANES):
                nc.gpsimd.memset(f32(rows[q][0][:, :, F:F + 1]), 1.0)
                nc.gpsimd.memset(f32(rows[q][0][:, :, F + 1:F + 2]), 0.0)
                nc.gpsimd.memset(f32(rows[q][1][:, :, F:F + 2]), 0.0)
            nc.gpsimd.memset(f32(wp[0][:, :, F:F + 2]), 0.0)
            nc.gpsimd.memset(f32(wp[1][:, :, F:F + 2]), 0.0).then_inc(const_set, 1)
            pool.wait_ge(const_set, 2)

            def own(q, name, it):
                pool.wait_ge(*after(name, q, it))

            def root(eps):
                def step(q, it):
                    own(q, eps, it)
                    nc.gpsimd.tensor_tensor(col(q, RS), col(q, VE), minus_half[:, :], ALU.pow).then_inc(gp_done[q], 1)
                return step

            windows(pool, "pool", ORDER_GP, {
                **elementwise(pool, nc.gpsimd, gp_done), "rsh": root("epsh"), "rs1": root("eps1"),
                "rs2": root("eps2"), "rs3": root("eps3"), "rs4": root("eps4")})


def kernel(**inputs):
    import numpy as _np
    import concourse.bacc as _bacc
    from concourse import mybir as _mybir
    from concourse.bass_utils import run_bass_kernel_spmd as _run

    a = {k: _np.asarray(v) for k, v in inputs.items()}
    laid = {
        "x": a["x"], "adjT": a["adj"].transpose(0, 2, 1),
        "W1T": a["L0_gnn_W1"].T, "b1": a["L0_gnn_b1"], "gamma": a["L0_gnn_gamma"].reshape(-1, 128).T,
        "beta": a["L0_gnn_beta"].reshape(-1, 128).T, "W2T": a["L0_gnn_W2"].T, "b2": a["L0_gnn_b2"],
        "C1": a["L1_gnn_W1"], "c1": a["L1_gnn_b1"].reshape(-1, 128).T,
        "C2": a["L1_gnn_W2"], "c2": a["L1_gnn_b2"].reshape(-1, 128).T,
        "C3": a["L1_gnn_W3"], "c3": a["L1_gnn_b3"], "WT": a["L2_gnn_W"].T, "w": a["L3_gnn_w"], "a": a["L3_gnn_a"],
    }
    nc = _bacc.Bacc("TRN2", target_bir_lowering=False, num_devices=1)
    arrays, args = {}, []
    for name, v in laid.items():
        v = _np.ascontiguousarray(v)
        arrays[f"in_{name}_dram"] = v
        args.append(nc.dram_tensor(f"in_{name}_dram", v.shape, _mybir.dt.from_np(v.dtype), kind="ExternalInput").ap())
    args.append(nc.dram_tensor("out_0_dram", a["x"].shape, _mybir.dt.from_np(_np.dtype("float32")),
                               kind="ExternalOutput").ap())
    graph_layers(nc, *args)
    r = _run(nc, [arrays], core_ids=[0])
    return r.results[0]["out_0_dram"]
```
